# Optimizing a Trainium2 kernel written in Bass

```python
import numpy as np
import jax
import jax.numpy as jnp

def _softmax(x, axis=-1):
    return jax.nn.softmax(x, axis=axis)
def _gelu(x):
    return jax.nn.gelu(x, approximate=True)
def _silu(x):
    return jax.nn.silu(x)
def _sigmoid(x):
    return jax.nn.sigmoid(x)
def _layernorm(x, axis=-1, eps=1e-5):
    m = jnp.mean(x, axis=axis, keepdims=True)
    v = jnp.var(x, axis=axis, keepdims=True)
    return (x - m) / jnp.sqrt(v + eps)
def _scatter_add(tgt, idx, src, axis=0):
    return tgt.at[idx].add(src)
def _segment_sum(src, seg, n):
    return jax.ops.segment_sum(src, seg, n)

kernel_name = 'mk_adj_resnorm_d2_adj_64_b86e5b'

def setup_inputs(seed: int = 0):
    np.random.seed(seed)
    _w = jnp.asarray
    def _rec_inputs():
        import jax
        import jax.numpy as jnp
        _gk = jax.random.key(seed)
        x = -9.806e-05 + 1 * jax.random.normal(jax.random.fold_in(_gk, 1), (8192, 64), jnp.float32)
        _a = jax.random.bernoulli(jax.random.fold_in(_gk, 2), 0.00195312, (8192, 8192))
        adj = _a.astype(jnp.int32)
        return x, adj
    x, adj = _rec_inputs()
    def _L0_gnn_setup():
        import jax, jax.numpy as jnp
        import numpy as np
        ALPHA = 0.2
        NEG_BIG = -9000000000000000.0
        key = jax.random.key(seed)
        k1, k2, k3, k4, k5 = jax.random.split(key, 5)
        N, M, F_in, F_out = (8192, 8192, 64, 64)
        item_embs = jax.random.normal(k1, (N, F_in), dtype=jnp.float32)
        entity_embs = jax.random.normal(k2, (M, F_in), dtype=jnp.float32)
        adj = jax.random.randint(k3, (N, M), 0, 2, dtype=jnp.int32)
        W = jax.random.normal(k4, (F_in, F_out), dtype=jnp.float32)
        a = jax.random.normal(k5, (2 * F_out, 1), dtype=jnp.float32)
        return {'item_embs': item_embs, 'entity_embs': entity_embs, 'adj': adj, 'W': W, 'a': a}
    _L0_gnn_all = _L0_gnn_setup()
    _L0_gnn_in = {k: v for k, v in _L0_gnn_all.items() if k in ('entity_embs', 'W', 'a', )}
    del _L0_gnn_all

    def _L1_gnn_setup():
        import jax, jax.numpy as jnp
        import numpy as np
        N = 20000
        F = 64
        O = 64
        key = jax.random.key(seed)
        k1, k2, k3 = jax.random.split(key, 3)
        x = jax.random.normal(k1, (N, F), dtype=jnp.float32)
        adj = jax.random.randint(k2, (N, N), 0, 2, dtype=jnp.int32)
        stdv = float(np.sqrt(6.0 / (2 * F + O)))
        weight = jax.random.uniform(k3, (2 * F, O), dtype=jnp.float32, minval=-stdv, maxval=stdv)
        bias = jnp.zeros((O,), dtype=jnp.float32)
        return {'x': x, 'adj': adj, 'weight': weight, 'bias': bias}
    _L1_gnn_all = _L1_gnn_setup()
    _L1_gnn_in = {k: v for k, v in _L1_gnn_all.items() if k in ('weight', 'bias', )}
    del _L1_gnn_all

    return {
        "x": x,
        "adj": adj,
        "L0_gnn_entity_embs": _L0_gnn_in["entity_embs"],
        "L0_gnn_W": _L0_gnn_in["W"],
        "L0_gnn_a": _L0_gnn_in["a"],
        "L1_gnn_weight": _L1_gnn_in["weight"],
        "L1_gnn_bias": _L1_gnn_in["bias"],
    }

def reference(x, adj, L0_gnn_entity_embs, L0_gnn_W, L0_gnn_a, L1_gnn_weight, L1_gnn_bias):
    import jax
    import jax.numpy as jnp
    def _L0_gnn_ref(item_embs, entity_embs, adj, W, a):
        import jax, jax.numpy as jnp
        import numpy as np
        ALPHA = 0.2
        NEG_BIG = -9000000000000000.0
        F_out = W.shape[1]
        Wh = item_embs @ W
        We = entity_embs @ W
        a1 = a[:F_out, 0]
        a2 = a[F_out:, 0]
        scores = (Wh @ a1)[:, None] + (We @ a2)[None, :]
        e = jnp.where(scores > 0, scores, ALPHA * scores)
        e = jnp.where(adj > 0, e, NEG_BIG)
        attention = jax.nn.softmax(e, axis=1)
        entity_emb_weighted = attention @ entity_embs
        h_prime = entity_emb_weighted + item_embs
        return jax.nn.elu(h_prime)

    def _L1_gnn_ref(x, adj, weight, bias):
        import jax, jax.numpy as jnp
        import numpy as np
        N = 20000
        F = 64
        O = 64
        a = (adj == 1).astype(x.dtype)
        deg = jnp.sum(a, axis=1, keepdims=True)
        x1 = a @ x / deg
        n_x = jnp.concatenate([x1, x], axis=1)
        return n_x @ weight + bias

    x = _layernorm(x + _L0_gnn_ref(x, L0_gnn_entity_embs, adj, L0_gnn_W, L0_gnn_a), axis=-1)
    x = _layernorm(x + _L1_gnn_ref(x, adj, L1_gnn_weight, L1_gnn_bias), axis=-1)
    return x


_drawn_inputs = setup_inputs


def setup_inputs(seed=0):
    import zlib

    import numpy as np

    out = dict(_drawn_inputs(seed))
    spreads = {'L1_gnn_bias': (0.0, 0.1)}
    factors = {}
    for name, (base, spread) in spreads.items():
        noise = np.random.default_rng([zlib.crc32(name.encode()), seed]).standard_normal(out[name].shape)
        drawn = base * np.exp(spread * noise) if base else spread * noise
        out[name] = jnp.asarray(drawn.astype(out[name].dtype))
    for name, factor in factors.items():
        out[name] = (out[name] * factor).astype(out[name].dtype)
    return out
```

```python
from contextlib import ExitStack

import concourse.bass as bass
from concourse import mybir

F32 = mybir.dt.float32
BF16 = mybir.dt.bfloat16
F16 = mybir.dt.float16
I16 = mybir.dt.int16
I32 = mybir.dt.int32
FP8 = mybir.dt.float8e4
ALU = mybir.AluOpType
ACT = mybir.ActivationFunctionType
AX = mybir.AxisListType
RMAX = bass.bass_isa.ReduceOp.max

P = 128
N = 8192
F = 64
TILES = N // P
IB = 1024
BLOCKS = N // IB
IT = IB // P
PAIR = 2
PAIRS = 4
OCT = PAIR * PAIRS
UNIT = 32
OPU = UNIT // OCT
OPB = TILES // OCT
OCTS = BLOCKS * OPB
RING = 6
PW = PAIR * IB
FE = F + 1
XW = 2 * F + 2
XU = 2 * F + 1
BIG = float(2 ** 17)
SLOPE = 0.2
REST = 1.0 - SLOPE
CODES = 32760.0
LO = 2048.0
EPS = 1e-5
FREE = 2
HALF = 512


def gnn_program(nc, x_t, adj_t, ent_t, w_t, a_col, wt1, bias1, out):
    s_row = nc.dram_tensor("s_row", (TILES, P), F32, kind="Internal").ap()
    edges = nc.dram_tensor("edges", (OCTS * PAIRS, P, PW // 2), I16, kind="Internal").ap()
    x16_d = nc.dram_tensor("x16_d", (BLOCKS, P, IT * XW), F16, kind="Internal").ap()
    x1_d = nc.dram_tensor("x1_d", (BLOCKS, P, IT * F), F32, kind="Internal").ap()

    ctx = ExitStack()
    with ctx:
        def sb(name, shape, dt):
            return ctx.enter_context(nc.sbuf_tensor(name, shape, dt))

        def sem(name):
            return ctx.enter_context(nc.semaphore(name))

        off = sb("off", [P, RING * OCT * IB], BF16)
        adjb = sb("adjb", [P, PAIRS, PW], I32)
        edge = sb("edge", [P, PAIRS, PW], FP8)
        cand = sb("cand", [P, PW], I16)
        best = sb("best", [P, PW], I16)
        prob = sb("prob", [P, 2, IB], F32)
        ent = sb("ent", [P, TILES, FE], F32)
        s_bc = sb("s_bc", [P, 2 * IB], F32)
        rows = sb("rows", [3, 2, IB], BF16)
        s_col = sb("s_col", [P, TILES], F32)
        code = sb("code", [P, TILES], F32)
        t_lo = sb("t_lo", [P, TILES], F32)
        t_hi = sb("t_hi", [P, TILES], F32)
        ident = sb("ident", [P, P], F32)
        ident16 = sb("ident16", [P, P], BF16)
        negbig = sb("negbig", [P, P], BF16)
        onesr = sb("onesr", [3, P], BF16)
        mean_e = sb("mean_e", [P, F], F32)
        wa = sb("wa", [P, 2, F], F32)
        small = sb("small", [P, 16], F32)
        stat = sb("stat", [P, 5, IT], F32)
        shift = sb("shift", [P, IT], F32)
        mom = sb("mom", [P, 8, IT], F32)
        half = sb("half", [P, IT], F32)
        s_rows = sb("s_rows", [TILES, P], F32)
        ones = sb("ones", [P, P], F32)
        parts = sb("parts", [P, 3, IT], BF16)
        partT = sb("partT", [3 * IT, P], BF16)
        maxes = sb("maxes", [P, 2, IT], F32)
        decay = sb("decay", [P, IT], F32)
        acc0 = sb("acc0", [P, IT, FE], F32)
        acc1 = sb("acc1", [P, IT, FE], F32)
        xblk = sb("xblk", [P, IT, F], F32)
        ya = sb("ya", [P, IT, F], F32)
        yb = sb("yb", [P, IT, F], F32)
        x16 = sb("x16", [P, IT, XW], F16)
        wt_s = sb("wt_s", [P, F], F32)
        bias_s = sb("bias_s", [P, F], F32)
        w_s = sb("w_s", [F, F], F32)
        a_s = sb("a_s", [F, 2], F32)
        a_bc = sb("a_bc", [F, 2, P], F32)
        x_all = off[:, 0:2 * TILES * F].bitcast(F32).rearrange("p (t f) -> p t f", f=F)
        e_all = off[:, 2 * TILES * F:4 * TILES * F].bitcast(F32).rearrange("p (t f) -> p t f", f=F)
        tmp = off[:, 4 * TILES * F:6 * TILES * F].bitcast(F32).rearrange("p (t f) -> p t f", f=F)
        EW = OCT * IB
        edge2 = off[:, 0:OPB * EW // 2].bitcast(FP8).rearrange("p (v n) -> p v n", v=OPB)
        x16_all = adjb[:, 0:3, :].rearrange("p a b -> p (a b)")[:, 0:TILES * XW // 2].bitcast(F16)\
            .rearrange("p (b t w) -> p b t w", b=BLOCKS, t=IT)
        bestf = cand[:, :].bitcast(F32)
        agg = ent[:, 0:18, :].rearrange("p a b -> p (a b)")[:, 0:9 * XU].rearrange("p (t w) -> p t w", t=9)
        nx = prob[:, 0, :].rearrange("p (t w) -> p t w", t=IT)
        nxT = prob[:, 1, :]

        ps = ctx.enter_context(nc.psum_tensor("ps", [P, 8, HALF], F32))
        score = [ps[:, 2 * n:2 * n + 2, :].rearrange("p a b -> p (a b)") for n in range(2)]
        sums = ps[:, 4:6, 0:4 * FE].rearrange("p a (t w) -> p a t w", t=4)
        sums_flat = ps[:, 4:6, 0:4 * FE]
        turn = ps[:, 6:8, :].rearrange("p a (t w) -> p (a t) w", w=P)
        turn16 = ps[0:3 * IT, 6, 0:HALF].bitcast(BF16)[:, 0:P]
        agg_ps = [ps[:, 3 * n:3 * n + 3, 0:3 * XU] for n in range(2)]

        ld_in = sem("ld_in")
        ld_x = sem("ld_x")
        ld_w = sem("ld_w")
        prep = sem("prep")
        pe_prep = sem("pe_prep")
        const_in = sem("const_in")
        srow_out = sem("srow_out")
        srow_tile = sem("srow_tile")
        pool_c = sem("pool_c")
        range_in = sem("range_in")
        range_out = sem("range_out")
        sbc_ld = sem("sbc_ld")
        adj_ld = [sem(f"adj_ld{k}") for k in range(PAIRS)]
        edge_st = [sem(f"edge_st{k}") for k in range(PAIRS)]
        off_in = sem("off_in")
        cand_in = sem("cand_in")
        best_up = sem("best_up")
        best_clear = sem("best_clear")
        pair_done = sem("pair_done")
        oct_done = sem("oct_done")
        stat_step = sem("stat_step")
        epi_step = sem("epi_step")
        fin_step = sem("fin_step")
        epi_a = sem("epi_a")
        epi_b = sem("epi_b")
        best_in = sem("best_in")
        best_T = sem("best_T")
        parts_in = sem("parts_in")
        parts_T = sem("parts_T")
        partT_in = sem("partT_in")
        rows_ld = sem("rows_ld")
        rows_due = sem("rows_due")
        shift_in = sem("shift_in")
        decay_in = sem("decay_in")
        relu_in = sem("relu_in")
        score_in = sem("score_in")
        prob_in = sem("prob_in")
        sums_free = sem("sums_free")
        xblk_ld = sem("xblk_ld")
        elu_in = sem("elu_in")
        elu_out = sem("elu_out")
        var_in = sem("var_in")
        var_out = sem("var_out")
        x16_in = sem("x16_in")
        x16_st = sem("x16_st")
        x1_st = sem("x1_st")
        x1_free = sem("x1_free")
        e2_ld = [sem(f"e2_ld{v}") for v in range(OPB)]
        x2_ld = [sem(f"x2_ld{b}") for b in range(BLOCKS)]
        e2_used = sem("e2_used")
        agg_free = sem("agg_free")
        nx_ld = sem("nx_ld")
        nx_in = sem("nx_in")
        nx_x_in = sem("nx_x_in")
        nx_T = sem("nx_T")
        nxT_in = sem("nxT_in")
        y_ps = sem("y_ps")
        out_in = sem("out_in")
        out_st = sem("out_st")


        block = ctx.enter_context(nc.Block())

        def whole(ap):
            return ap.rearrange("a p n -> (a p) n")

        def over_f(ap):
            return ap.unsqueeze(2).to_broadcast([P, IT, F])

        def over_t(ap):
            return ap.unsqueeze(1).to_broadcast([P, IT, F])

        def pair_of(o, k):
            return off[:, bass.ds((o % RING) * (OCT * IB) + k * PW, PW)]

        def edge_load(sp, b, v):
            sp.dma_start(edge2[:, v, :].bitcast(I16).rearrange("p (k n) -> p k n", k=PAIRS),
                         edges[bass.ds(b * (OPB * PAIRS) + v * PAIRS, PAIRS)]
                         .rearrange("k p n -> p k n")).then_inc(e2_ld[v], 16)

        @block.sync
        def _(sp):
            sp.dma_start(e_all, ent_t.rearrange("p (t f) -> p t f", f=F)).then_inc(ld_in, 16)
            sp.dma_start(w_s[:], w_t).then_inc(ld_in, 16)
            sp.dma_start(a_s[:], a_col).then_inc(ld_in, 16)
            sp.dma_start(x_all, x_t.rearrange("p (t f) -> p t f", f=F)).then_inc(ld_x, 16)
            for k in range(PAIRS):
                sp.dma_start(adjb[:, k, :], adj_t[k]).then_inc(adj_ld[k], 16)
            sp.dma_start(wt_s[:], wt1).then_inc(ld_w, 16)
            sp.dma_start(bias_s[:], bias1.to_broadcast([P, F])).then_inc(ld_w, 16)
            sp.wait_ge(srow_tile, 1)
            sp.dma_start(s_row, s_rows[:, :]).then_inc(srow_out, 16)
            with sp.Fori(0, OCTS - 1) as o:
                for k in range(PAIRS):
                    sp.wait_ge(pair_done, o * PAIRS + (k + 1))
                    sp.dma_start(adjb[:, k, :], whole(adj_t[bass.ds(o * PAIRS + (k + PAIRS), 1)]))\
                      .then_inc(adj_ld[k], 16)
                    sp.dma_start(whole(edges[bass.ds(o * PAIRS + k, 1)]), edge[:, k, :].bitcast(I16))\
                      .then_inc(edge_st[k], 16)
            for k in range(PAIRS):
                sp.wait_ge(pair_done, (OCTS - 1) * PAIRS + k + 1)
                sp.dma_start(edges[(OCTS - 1) * PAIRS + k], edge[:, k, :].bitcast(I16)).then_inc(edge_st[k], 16)
            for b in range(BLOCKS):
                if b == BLOCKS - 1:
                    sp.wait_ge(oct_done, OCTS)
                    for k in range(PAIRS):
                        sp.wait_ge(edge_st[k], 16 * OCTS)
                    for v in range(OPB):
                        edge_load(sp, 0, v)
                sp.wait_ge(x16_st, 16 * (b + 1))
                sp.dma_start(x16_all[:, b], x16_d[b].rearrange("p (t w) -> p t w", t=IT)).then_inc(x2_ld[b], 16)
            with sp.Fori(1, BLOCKS) as b:
                for v in range(OPB):
                    sp.wait_ge(e2_used, (b - 1) * OPB + (v + 1))
                    edge_load(sp, b, v)

        @block.gpsimd
        def _(pool):
            pool.memset(ident[:], 0.0).then_inc(pool_c, 1)
            pool.memset(half[:], -0.5).then_inc(pool_c, 1)
            pool.wait_ge(pool_c, 2)
            pool.affine_select(out=ident[:], in_=ident[:], compare_op=ALU.not_equal, fill=1.0, base=0,
                               pattern=[[-1, P]], channel_multiplier=1).then_inc(pool_c, 1)
            pool.wait_ge(range_in, 2)
            pool.partition_all_reduce(small[:, 2:4], small[:, 0:2], P, RMAX).then_inc(range_out, 1)

            def load_s(b):
                pool.dma_start(s_bc[:, bass.ds((b % 2) * IB, IB)],
                               s_row.rearrange("(b t) p -> b (t p)", b=BLOCKS)[bass.ds(b, 1), :]
                               .to_broadcast([P, IB])).then_inc(sbc_ld, 16)

            def load_rows(b, c):
                pool.wait_ge(partT_in, 2 * b + c + 1)
                pool.sem_inc(rows_due, 1)
                pool.dma_start(rows[:, c, :].rearrange("k (t p) -> k t p", p=P), partT[:, :])\
                    .then_inc(rows_ld, 16)

            def load_x(b):
                pool.dma_start(xblk[:].rearrange("p t f -> p (t f)"),
                               x_t.rearrange("p (b n) -> b p n", b=BLOCKS)[bass.ds(b, 1)]
                               .rearrange("a p n -> (a p) n")).then_inc(xblk_ld, 16)

            def finish_x1(b):
                pool.wait_ge(var_in, b + 1)
                pool.tensor_tensor(mom[:, 7, :], mom[:, 6, :], half[:, :], ALU.pow).then_inc(var_out, 1)
                pool.wait_ge(x16_in, b + 1)
                pool.dma_start(whole(x16_d[bass.ds(b, 1)]),
                               x16[:, :, :].rearrange("p t w -> p (t w)")).then_inc(x16_st, 16)
                pool.dma_start(whole(x1_d[bass.ds(b, 1)]),
                               ya[:, :, :].rearrange("p t f -> p (t f)")).then_inc(x1_st, 16)
                pool.wait_ge(x16_st, b * 16 + 16)
                pool.wait_ge(x1_st, b * 16 + 16)
                pool.sem_inc(x1_free, 1)

            pool.sem_inc(x1_free, 1)
            pool.wait_ge(srow_out, 16)
            load_s(0)
            pool.wait_ge(sbc_ld, 16)
            load_s(1)
            load_x(0)
            load_rows(0, 0)
            load_rows(0, 1)

            def block_of(b, more):
                load_rows(b, 0)
                if more:
                    pool.wait_ge(sbc_ld, b * 16 + 16)
                    pool.wait_ge(oct_done, b * OPB)
                    load_s(b + 1)
                load_rows(b, 1)
                finish_x1(b - 1)
                load_x(b)

            with pool.Fori(1, BLOCKS - 1) as b:
                block_of(b, True)
            block_of(BLOCKS - 1, False)
            finish_x1(BLOCKS - 1)
            pool.wait_ge(x1_st, 16 * BLOCKS)
            for b in range(BLOCKS):
                pool.wait_ge(var_in, BLOCKS + b + 1)
                pool.tensor_tensor(mom[:, 7, :], mom[:, 6, :], half[:, :], ALU.pow).then_inc(var_out, 1)

        @block.vector
        def _(dve):
            V = nc.vector
            at = [0]

            def link(ins, sem_, base=0):
                at[0] += 1
                ins.then_inc(sem_, 1)
                dve.wait_ge(sem_, base + at[0])

            V.memset(a_bc[:].rearrange("p a b -> p (a b)"), 1.0).then_inc(prep, 1)
            V.memset(onesr[:], 1.0).then_inc(prep, 1)
            V.memset(ones[:], 1.0).then_inc(prep, 1)
            V.memset(ent[:, :, F:FE], 1.0).then_inc(prep, 1)
            V.memset(x16[:, :, 2 * F:2 * F + 1], 1.0).then_inc(prep, 1)
            V.memset(x16[:, :, 2 * F + 1:XW], 0.0).then_inc(prep, 1)
            V.memset(sums_flat, 0.0).then_inc(sums_free, 1)
            at[0] = 6
            dve.wait_ge(pool_c, 3)
            V.tensor_scalar(negbig[:], ident[:], -BIG, None, ALU.mult).then_inc(prep, 1)
            V.tensor_copy(ident16[:], ident[:]).then_inc(prep, 1)
            at[0] = 8
            dve.wait_ge(prep, 8)
            dve.wait_ge(ld_in, 48)
            for k in range(2):
                link(V.tensor_scalar(a_bc[:, k, :], a_bc[:, k, :], a_s[:, k:k + 1], None, ALU.mult), prep)
            V.tensor_copy(ent[:, :, 0:F], e_all).then_inc(const_in, 1)
            dve.wait_ge(pe_prep, 1)
            link(V.tensor_copy(wa[:], ps[:, 6, 0:2 * F].rearrange("p (k f) -> p k f", k=2)), prep)

            def over_tiles(ap):
                return ap.unsqueeze(1).to_broadcast([P, TILES, F])

            link(V.tensor_tensor(tmp, e_all, over_tiles(wa[:, 1, :]), ALU.mult), prep)
            link(V.tensor_reduce(t_lo[:], tmp, AX.X, ALU.add), prep)
            V.tensor_reduce(small[:, 0:1], t_lo[:], AX.X, ALU.max).then_inc(range_in, 1)
            link(V.tensor_reduce(small[:, 8:9], t_lo[:], AX.X, ALU.min), prep)
            V.tensor_scalar(small[:, 1:2], small[:, 8:9], -1.0, None, ALU.mult).then_inc(range_in, 1)
            dve.wait_ge(ld_x, 16)
            link(V.tensor_tensor(tmp, x_all, over_tiles(wa[:, 0, :]), ALU.mult), prep)
            link(V.tensor_reduce(s_col[:], tmp, AX.X, ALU.add), prep)
            V.tensor_reduce(mean_e[:], e_all.rearrange("p t f -> p f t"), AX.X, ALU.add).then_inc(const_in, 1)
            dve.wait_ge(pe_prep, 2)
            V.tensor_copy(s_rows[:, :], ps[0:TILES, 7, 0:P]).then_inc(srow_tile, 1)
            dve.wait_ge(range_out, 1)
            link(V.tensor_tensor(small[:, 4:5], small[:, 2:3], small[:, 3:4], ALU.add), prep)
            link(V.tensor_scalar(small[:, 5:6], small[:, 4:5], 1.0 / CODES, 1e-30, ALU.mult, ALU.max), prep)
            link(V.reciprocal(small[:, 6:7], small[:, 5:6]), prep)
            link(V.tensor_tensor(small[:, 9:10], small[:, 3:4], small[:, 5:6], ALU.add), prep)
            link(V.tensor_scalar(small[:, 7:8], small[:, 9:10], -1.0, None, ALU.mult), prep)
            link(V.tensor_scalar(code[:], t_lo[:], small[:, 3:4], small[:, 6:7], ALU.add, ALU.mult), prep)
            link(V.tensor_scalar(code[:], code[:], 2.0, None, ALU.add), prep)
            link(V.tensor_scalar(t_hi[:], t_lo[:], REST, None, ALU.mult), prep)
            V.tensor_scalar(t_lo[:], t_lo[:], SLOPE, None, ALU.mult).then_inc(const_in, 1)
            dve.wait_ge(pe_prep, 3)
            link(V.tensor_scalar(mean_e[:], ps[:, 6, 2 * F:3 * F], 1.0 / N, None, ALU.mult), prep)

            def sweep_a(o, c, oo, ring_free=True, first=False):
                if ring_free:
                    dve.wait_ge(oct_done, o - (RING - 1))
                for k in range(PAIRS):
                    if not first:
                        dve.wait_ge(edge_st[k], o * 16)
                    dve.wait_ge(adj_ld[k], o * 16 + 16)
                    pair = pair_of(o, k)
                    V.tensor_scalar(pair, adjb[:, k, :], 0.0, None, ALU.is_le).then_inc(off_in, 1)
                    V.tensor_scalar(edge[:, k, :], adjb[:, k, :], 1.0, None, ALU.is_equal,
                                    saturate=False).then_inc(pair_done, 1)
                    dve.wait_ge(off_in, o * PAIRS + (k + 1))
                    if not first or k:
                        dve.wait_ge(best_up, o * PAIRS + k)
                    for n in range(PAIR):
                        tile_off = off[:, bass.ds((o % RING) * (OCT * IB) + (k * PAIR + n) * IB, IB)]
                        jt = (c * OPU + oo) * OCT + (k * PAIR + n)
                        V.tensor_scalar(cand[:, n * IB:(n + 1) * IB], tile_off, 0.0,
                                        code[:, bass.ds(jt, 1)], ALU.is_equal, ALU.mult).then_inc(cand_in, 1)
                    dve.wait_ge(cand_in, o * OCT + (k + 1) * PAIR)
                    V.tensor_tensor(best[:], best[:], cand[:], ALU.max).then_inc(best_up, 1)

            STATS = 8

            def stats(b, c):
                u = 2 * b + c
                at[0] = 0

                def step(ins):
                    link(ins, stat_step, u * STATS)

                dve.wait_ge(best_up, (u + 1) * (OPU * PAIRS))
                V.tensor_tensor(bestf, best[:, 0:IB], best[:, IB:PW], ALU.max).then_inc(best_in, 1)
                dve.wait_ge(best_T, u + 1)
                step(V.tensor_reduce(stat[:, 0, :], turn, AX.X, ALU.max))
                step(V.tensor_scalar(stat[:, 1, :], stat[:, 0, :], small[:, 5:6], small[:, 7:8],
                                     ALU.mult, ALU.add))
                s_b = s_col[:, bass.ds(b * IT, IT)]
                step(V.tensor_tensor(stat[:, 2, :], stat[:, 1, :], s_b, ALU.add))
                step(V.scalar_tensor_tensor(maxes[:, c, :], stat[:, 2, :], SLOPE, stat[:, 2, :],
                                            ALU.mult, ALU.max))
                step(V.scalar_tensor_tensor(stat[:, 3, :], s_b, SLOPE, maxes[:, c, :],
                                            ALU.mult, ALU.subtract))
                step(V.tensor_copy(parts[:, 0, :], stat[:, 3, :]))
                step(V.tensor_tensor(stat[:, 4, :], stat[:, 3, :], parts[:, 0, :], ALU.subtract))
                step(V.tensor_copy(parts[:, 1, :], stat[:, 4, :]))
                V.tensor_tensor(parts[:, 2, :], stat[:, 4, :], parts[:, 1, :], ALU.subtract).then_inc(parts_in, 1)
                if c == 1:
                    V.tensor_tensor(shift[:], maxes[:, 0, :], maxes[:, 1, :], ALU.subtract).then_inc(shift_in, 1)
                dve.wait_ge(parts_T, u + 1)
                if not (isinstance(u, int) and u == 0):
                    dve.wait_ge(rows_ld, u * 16)
                V.tensor_copy(partT[:, :], turn16).then_inc(partT_in, 1)
                assert at[0] == STATS

            def evac0(b):
                dve.wait_ge(oct_done, b * OPB + OPU)
                V.tensor_copy(acc0[:, :, :].rearrange("p (a t) w -> p a t w", a=2), sums).then_inc(epi_a, 1)
                dve.wait_ge(epi_a, b + 1)
                V.memset(sums_flat, 0.0).then_inc(sums_free, 1)

            EPI = 16

            def evac1(b, zero):
                at[0] = 0

                def step(ins):
                    link(ins, epi_step, b * EPI)

                dve.wait_ge(decay_in, b + 1)
                step(V.tensor_tensor(acc0[:, :, :], acc0[:, :, :],
                                     decay[:, :].unsqueeze(2).to_broadcast([P, IT, FE]), ALU.mult))
                dve.wait_ge(oct_done, b * OPB + OPB)
                step(V.tensor_tensor(acc1[:, :, :].rearrange("p (a t) w -> p a t w", a=2), sums,
                                     acc0[:, :, :].rearrange("p (a t) w -> p a t w", a=2), ALU.add))
                if zero:
                    V.memset(sums_flat, 0.0).then_inc(sums_free, 1)
                else:
                    for n in range(2):
                        dve.wait_ge(prob_in, BLOCKS * TILES + FREE)
                        V.memset(agg_ps[n], 0.0).then_inc(agg_free, 1)
                den = acc1[:, :, F:FE].rearrange("p t o -> p (t o)")
                step(V.tensor_scalar(mom[:, 0, :], den, 0.0, None, ALU.is_equal))
                step(V.tensor_tensor(mom[:, 1, :], den, mom[:, 0, :], ALU.add))
                step(V.reciprocal(mom[:, 2, :], mom[:, 1, :]))
                dve.wait_ge(x1_free, b + 1)
                step(V.tensor_tensor(ya[:], acc1[:, :, 0:F], over_f(mom[:, 2, :]), ALU.mult))
                step(V.tensor_tensor(yb[:], over_t(mean_e[:]), over_f(mom[:, 0, :]), ALU.mult))
                step(V.tensor_tensor(ya[:], ya[:], yb[:], ALU.add))
                dve.wait_ge(xblk_ld, b * 16 + 16)
                step(V.tensor_tensor(ya[:], ya[:], xblk[:], ALU.add))
                V.tensor_scalar(yb[:], ya[:], 0.0, None, ALU.min).then_inc(elu_in, 1)

            def norm(step, b):
                step(V.tensor_reduce(mom[:, 3, :], ya[:], AX.X, ALU.add))
                step(V.tensor_scalar(mom[:, 4, :], mom[:, 3, :], 1.0 / F, None, ALU.mult))
                step(V.tensor_tensor(ya[:], ya[:], over_f(mom[:, 4, :]), ALU.subtract))
                step(V.tensor_tensor(yb[:], ya[:], ya[:], ALU.mult))
                step(V.tensor_reduce(mom[:, 5, :], yb[:], AX.X, ALU.add))
                V.tensor_scalar(mom[:, 6, :], mom[:, 5, :], 1.0 / F, EPS, ALU.mult, ALU.add).then_inc(var_in, 1)
                dve.wait_ge(var_out, b + 1)

            def layer0_end(b):
                at[0] = 9

                def step(ins):
                    link(ins, epi_step, b * EPI)

                dve.wait_ge(elu_out, b + 1)
                step(V.scalar_tensor_tensor(ya[:], ya[:], 0.0, yb[:], ALU.max, ALU.add))
                step(V.scalar_tensor_tensor(ya[:], ya[:], -1.0, xblk[:], ALU.add, ALU.add))
                norm(step, b)
                V.tensor_tensor(ya[:], ya[:], over_f(mom[:, 7, :]), ALU.mult).then_inc(epi_b, 1)
                dve.wait_ge(epi_b, b * 3 + 1)
                V.tensor_copy(x16[:, :, 0:F], ya[:]).then_inc(epi_b, 1)
                dve.wait_ge(epi_b, b * 3 + 2)
                V.tensor_tensor(yb[:], ya[:], x16[:, :, 0:F], ALU.subtract).then_inc(epi_b, 1)
                dve.wait_ge(epi_b, b * 3 + 3)
                V.tensor_scalar(x16[:, :, F:2 * F], yb[:], LO, None, ALU.mult).then_inc(x16_in, 1)
                assert at[0] == EPI

            def clear_best(b):
                V.memset(best[:].bitcast(I32), 0).then_inc(best_clear, 1)
                dve.wait_ge(best_clear, b + 1)

            clear_best(0)
            sweep_a(0, 0, 0, False, True)
            with dve.Fori(1, OPU) as oo:
                sweep_a(oo, 0, oo, False)
            stats(0, 0)
            for oo in range(OPU):
                sweep_a(OPU + oo, 1, oo, OPU + oo >= RING)
            stats(0, 1)

            def block_of(b):
                clear_best(b)
                sweep_a(b * OPB, 0, 0, True)
                evac0(b - 1)
                with dve.Fori(1, OPU) as oo:
                    sweep_a(b * OPB + oo, 0, oo, True)
                stats(b, 0)
                sweep_a(b * OPB + OPU, 1, 0, True)
                evac1(b - 1, True)
                with dve.Fori(1, OPU) as oo:
                    sweep_a(b * OPB + OPU + oo, 1, oo, True)
                stats(b, 1)
                layer0_end(b - 1)

            with dve.Fori(1, BLOCKS) as b:
                block_of(b)
            last = BLOCKS - 1
            evac0(last)
            evac1(last, False)
            layer0_end(last)

            FIN = 10

            def layer1_end(b, n, more):
                at[0] = 0

                def step(ins):
                    link(ins, fin_step, b * FIN)

                dve.wait_ge(e2_used, (b + 1) * OPB)
                step(V.tensor_copy(agg.rearrange("p (a t) w -> p a (t w)", a=3), agg_ps[n]))
                if more:
                    V.memset(agg_ps[n], 0.0).then_inc(agg_free, 1)
                step(V.reciprocal(mom[:, 0, :], agg[:, 0:IT, 2 * F:XU].rearrange("p t o -> p (t o)")))
                if b == 0:
                    dve.wait_ge(x1_st, 16 * BLOCKS)
                else:
                    dve.wait_ge(out_st, b * 16)
                step(V.scalar_tensor_tensor(ya[:], agg[:, 0:IT, F:2 * F], 1.0 / LO, agg[:, 0:IT, 0:F],
                                            ALU.mult, ALU.add))
                V.tensor_tensor(nx[:, :, 0:F], ya[:], over_f(mom[:, 0, :]), ALU.mult).then_inc(nx_in, 1)
                dve.wait_ge(y_ps, b + 1)
                step(V.tensor_tensor(ya[:], ps[:, 6, :].rearrange("p (t f) -> p t f", f=F), xblk[:], ALU.add))
                step(V.tensor_tensor(ya[:], ya[:], over_t(bias_s[:]), ALU.add))
                norm(step, b + BLOCKS)
                V.tensor_tensor(ya[:], ya[:], over_f(mom[:, 7, :]), ALU.mult).then_inc(out_in, 1)
                assert at[0] == FIN

            dve.wait_ge(ld_w, 32)
            for b in range(BLOCKS):
                layer1_end(b, b % 2, b + 2 < BLOCKS)

        @block.scalar
        def _(act):
            A = nc.scalar

            def octet(b, c, oo):
                o = b * OPB + (c * OPU + oo)
                srow = s_bc[:, bass.ds((b % 2) * IB, IB)]

                def relu(t):
                    jt = (c * OPU + oo) * OCT + t
                    act.wait_ge(prob_in, o * OCT + (t + 1))
                    A.activation(score[t % 2], srow, ACT.Relu, scale=REST,
                                 bias=t_hi[:, bass.ds(jt, 1)]).then_inc(relu_in, 1)

                relu(0)
                for t in range(OCT):
                    if t + 1 < OCT:
                        relu(t + 1)
                    jt = (c * OPU + oo) * OCT + t
                    act.wait_ge(score_in, o * OCT + (t + 1))
                    A.activation(prob[:, t % 2, :], score[t % 2], ACT.Exp,
                                 bias=t_lo[:, bass.ds(jt, 1)]).then_inc(prob_in, 1)

            def exp_decay(b):
                act.wait_ge(shift_in, b + 1)
                A.activation(decay[:], shift[:], ACT.Exp).then_inc(decay_in, 1)

            def exp_elu(b):
                act.wait_ge(elu_in, b + 1)
                A.activation(yb[:], yb[:], ACT.Exp).then_inc(elu_out, 1)

            def block_of(b, elu):
                act.wait_ge(sbc_ld, b * 16 + 16)
                with act.Fori(0, OPU // 2) as oo:
                    octet(b, 0, oo)
                if elu:
                    exp_elu(b - 1)
                with act.Fori(OPU // 2, OPU) as oo:
                    octet(b, 0, oo)
                exp_decay(b)
                with act.Fori(0, OPU) as oo:
                    octet(b, 1, oo)

            act.sem_inc(prob_in, FREE)
            act.wait_ge(const_in, 3)
            act.wait_ge(pe_prep, 4)
            block_of(0, False)
            with act.Fori(1, BLOCKS) as b:
                block_of(b, True)
            exp_elu(BLOCKS - 1)
            act.wait_ge(x1_st, 16 * BLOCKS)
            for b in range(BLOCKS):
                if b:
                    act.wait_ge(out_in, b)
                    act.dma_start(out[b - 1], ya[:].rearrange("p t f -> p (t f)")).then_inc(out_st, 16)
                act.dma_start(xblk[:].rearrange("p t f -> p (t f)"), x1_d[b]).then_inc(nx_ld, 16)
                act.wait_ge(nx_ld, 16 * (b + 1))
                A.copy(nx[:, :, F:2 * F], xblk[:]).then_inc(nx_x_in, 1)
                act.wait_ge(nx_T, b + 1)
                A.copy(nxT, turn.rearrange("p t w -> p (t w)")).then_inc(nxT_in, 1)
            act.wait_ge(out_in, BLOCKS)
            act.dma_start(out[BLOCKS - 1], ya[:].rearrange("p t f -> p (t f)")).then_inc(out_st, 16)
            act.wait_ge(out_st, 16 * BLOCKS)

        @block.tensor
        def _(pe):
            M = nc.tensor.matmul
            pe.wait_ge(prep, 10)
            for k in range(2):
                ins = M(ps[:, 6, k * F:(k + 1) * F], a_bc[:, k, :], w_s[:, :], start=True, stop=True)
            ins.then_inc(pe_prep, 1)
            pe.wait_ge(prep, 16)
            nc.tensor.transpose(ps[0:TILES, 7, 0:P], s_col[:, :], ident[:, :]).then_inc(pe_prep, 1)
            pe.wait_ge(const_in, 2)
            M(ps[:, 6, 2 * F:3 * F], ones[:, :], mean_e[:, :], start=True, stop=True).then_inc(pe_prep, 1)
            for n in range(2):
                for h in range(2):
                    for q in range(HALF // P):
                        at = h * HALF + q * P
                        ins = M(score[n][:, at:at + P], ident16[:, :], negbig[:, :], start=q == 0, stop=True,
                                skip_group_check=True)
            ins.then_inc(pe_prep, 1)

            def turn_best(u):
                pe.wait_ge(best_in, u + 1)
                for t in range(IT):
                    ins = nc.tensor.transpose(turn[:, t, :], bestf[:, t * P:(t + 1) * P], ident[:, :])
                ins.then_inc(best_T, 1)

            def turn_parts(u):
                pe.wait_ge(parts_in, u + 1)
                nc.tensor.transpose(turn16, parts[:, :, :].rearrange("p k t -> p (k t)"),
                                    ident16[:, :]).then_inc(parts_T, 1)

            def octet(b, c, oo, then):
                o = b * OPB + (c * OPU + oo)

                def add(t):
                    if t == 0:
                        pe.wait_ge(rows_ld, (2 * b + c) * 16 + 16)
                    pe.wait_ge(relu_in, o * OCT + (t + 1))
                    for h in range(2):
                        M(score[t % 2][:, h * HALF:(h + 1) * HALF], negbig[:, :],
                          off[:, bass.ds((o % RING) * (OCT * IB) + t * IB + h * HALF, HALF)],
                          start=False, stop=True, skip_group_check=True)
                    for h in range(2):
                        ins = M(score[t % 2][:, h * HALF:(h + 1) * HALF], onesr[:, :],
                                rows[:, c, h * HALF:(h + 1) * HALF], start=False, stop=True,
                                skip_group_check=True)
                    ins.then_inc(score_in, 1)

                def weigh(t):
                    if t == 0:
                        pe.wait_ge(sums_free, 2 * b + c + 1)
                    pe.wait_ge(prob_in, o * OCT + (t + 1 + FREE))
                    jt = (c * OPU + oo) * OCT + t
                    for n in range(IT):
                        ins = M(sums[:, n // 4, n % 4, :], prob[:, t % 2, n * P:(n + 1) * P],
                                ent[:, bass.ds(jt, 1), :].rearrange("p a w -> p (a w)"),
                                start=False, stop=True, skip_group_check=True)
                    if t == OCT - 1:
                        ins.then_inc(oct_done, 1)

                add(0)
                for t in range(OCT):
                    if t + 1 < OCT:
                        add(t + 1)
                    weigh(t)
                    if t in then:
                        then[t]()

            def unit(b, c, more):
                u = 2 * b + c
                with pe.Fori(0, OPU - 1) as oo:
                    octet(b, c, oo, {})
                octet(b, c, OPU - 1, {1: lambda: turn_best(u + 1), 4: lambda: turn_parts(u + 1)} if more else {})

            turn_best(0)
            turn_parts(0)
            with pe.Fori(0, BLOCKS - 1) as b:
                unit(b, 0, True)
                unit(b, 1, True)
            unit(BLOCKS - 1, 0, True)
            unit(BLOCKS - 1, 1, False)

            def edges_of(b, n, then):
                pe.wait_ge(agg_free, b + 1)
                for v in range(OPB):
                    pe.wait_ge(e2_ld[v], b * 16 + 16)
                    pe.wait_ge(x2_ld[v], 16)
                    for t in range(OCT):
                        for m in range(IT):
                            ins = M(agg_ps[n][:, m // 3, (m % 3) * XU:(m % 3 + 1) * XU],
                                    edge2[:, v, t * IB + m * P:t * IB + (m + 1) * P],
                                    x16_all[:, v, t, 0:XU], start=False, stop=True, skip_group_check=True)
                    ins.then_inc(e2_used, 1)
                    if v in then:
                        then[v]()

            def turn_nx(b):
                pe.wait_ge(nx_in, b + 1)
                pe.wait_ge(nx_x_in, b + 1)
                for m in range(IT):
                    ins = nc.tensor.transpose(turn[:, m, :], nx[:, m, :], ident[:, :])
                ins.then_inc(nx_T, 1)

            def apply_weight(b):
                pe.wait_ge(nxT_in, b + 1)
                for m in range(IT):
                    ins = M(ps[:, 6, m * F:(m + 1) * F], nxT[:, m * P:(m + 1) * P], wt_s[:, :],
                            start=True, stop=True)
                ins.then_inc(y_ps, 1)

            edges_of(0, 0, {})
            for b in range(1, BLOCKS):
                edges_of(b, b % 2, {3: lambda: turn_nx(b - 1), 5: lambda: apply_weight(b - 1)})
            turn_nx(BLOCKS - 1)
            apply_weight(BLOCKS - 1)


def kernel(x, adj, L0_gnn_entity_embs, L0_gnn_W, L0_gnn_a, L1_gnn_weight, L1_gnn_bias):
    import numpy as np
    import concourse.bacc as bacc
    from concourse.bass_utils import run_bass_kernel_spmd

    def tiled(a):
        return np.ascontiguousarray(np.asarray(a).reshape(TILES, P, F).transpose(1, 0, 2)).reshape(P, TILES * F)

    adj_t = np.asarray(adj).reshape(BLOCKS, IB, OPB, PAIRS, PAIR, P).transpose(0, 2, 3, 5, 4, 1)
    arrays = {
        "x_t": tiled(x),
        "adj_t": np.ascontiguousarray(adj_t).reshape(OCTS * PAIRS, P, PW),
        "ent_t": tiled(L0_gnn_entity_embs),
        "w_t": np.ascontiguousarray(np.asarray(L0_gnn_W).T),
        "a_col": np.ascontiguousarray(np.asarray(L0_gnn_a).reshape(2, F).T),
        "wt1": np.ascontiguousarray(np.asarray(L1_gnn_weight)),
        "bias1": np.ascontiguousarray(np.asarray(L1_gnn_bias).reshape(1, F)),
    }
    nc = bacc.Bacc("TRN2", target_bir_lowering=False, num_devices=1)
    args = [nc.dram_tensor(k, a.shape, mybir.dt.from_np(a.dtype), kind="ExternalInput").ap()
            for k, a in arrays.items()]
    out = nc.dram_tensor("out", (BLOCKS, P, IT * F), F32, kind="ExternalOutput").ap()
    gnn_program(nc, *args, out)
    got = run_bass_kernel_spmd(nc, [arrays], core_ids=[0]).results[0]["out"]
    return np.ascontiguousarray(np.asarray(got).reshape(BLOCKS, P, IT, F).transpose(0, 2, 1, 3)).reshape(N, F)
```

```python
from contextlib import ExitStack

import concourse.bass as bass
from concourse import mybir

F32 = mybir.dt.float32
BF16 = mybir.dt.bfloat16
F16 = mybir.dt.float16
I16 = mybir.dt.int16
I32 = mybir.dt.int32
FP8 = mybir.dt.float8e4
ALU = mybir.AluOpType
ACT = mybir.ActivationFunctionType
AX = mybir.AxisListType
RMAX = bass.bass_isa.ReduceOp.max

P = 128
N = 8192
F = 64
TILES = N // P
IB = 1024
BLOCKS = N // IB
IT = IB // P
PAIR = 2
PAIRS = 4
OCT = PAIR * PAIRS
UNIT = 32
OPU = UNIT // OCT
OPB = TILES // OCT
OCTS = BLOCKS * OPB
RING = 6
PW = PAIR * IB
FE = F + 1
XW = 2 * F + 2
XU = 2 * F + 1
BIG = float(2 ** 17)
SLOPE = 0.2
REST = 1.0 - SLOPE
CODES = 32760.0
LO = 2048.0
EPS = 1e-5
FREE = 2
HALF = 512


def gnn_program(nc, x_t, adj_t, ent_t, w_t, a_col, wt1, bias1, out):
    s_row = nc.dram_tensor("s_row", (TILES, P), F32, kind="Internal").ap()
    edges = nc.dram_tensor("edges", (OCTS * PAIRS, P, PW // 2), I16, kind="Internal").ap()
    x16_d = nc.dram_tensor("x16_d", (BLOCKS, P, IT * XW), F16, kind="Internal").ap()
    x1_d = nc.dram_tensor("x1_d", (BLOCKS, P, IT * F), F32, kind="Internal").ap()

    ctx = ExitStack()
    with ctx:
        def sb(name, shape, dt):
            return ctx.enter_context(nc.sbuf_tensor(name, shape, dt))

        def sem(name):
            return ctx.enter_context(nc.semaphore(name))

        off = sb("off", [P, RING * OCT * IB], BF16)
        adjb = sb("adjb", [P, PAIRS, PW], I32)
        edge = sb("edge", [P, PAIRS, PW], FP8)
        cand = sb("cand", [P, PW], I16)
        best = sb("best", [P, PW], I16)
        prob = sb("prob", [P, 2, IB], F32)
        ent = sb("ent", [P, TILES, FE], F32)
        s_bc = sb("s_bc", [P, 2 * IB], F32)
        rows = sb("rows", [3, 2, IB], BF16)
        s_col = sb("s_col", [P, TILES], F32)
        code = sb("code", [P, TILES], F32)
        t_lo = sb("t_lo", [P, TILES], F32)
        t_hi = sb("t_hi", [P, TILES], F32)
        ident = sb("ident", [P, P], F32)
        ident16 = sb("ident16", [P, P], BF16)
        negbig = sb("negbig", [P, P], BF16)
        onesr = sb("onesr", [3, P], BF16)
        mean_e = sb("mean_e", [P, F], F32)
        wa = sb("wa", [P, 2, F], F32)
        small = sb("small", [P, 16], F32)
        stat = sb("stat", [P, 5, IT], F32)
        shift = sb("shift", [P, IT], F32)
        mom = sb("mom", [P, 8, IT], F32)
        half = sb("half", [P, IT], F32)
        s_rows = sb("s_rows", [TILES, P], F32)
        ones = sb("ones", [P, P], F32)
        parts = sb("parts", [P, 3, IT], BF16)
        partT = sb("partT", [3 * IT, P], BF16)
        maxes = sb("maxes", [P, 2, IT], F32)
        decay = sb("decay", [P, IT], F32)
        acc0 = sb("acc0", [P, IT, FE], F32)
        accT = sb("accT", [FE, IB], F32)
        xblk = sb("xblk", [P, IT, F], F32)
        ya = sb("ya", [P, IT, F], F32)
        yb = sb("yb", [P, IT, F], F32)
        x16 = sb("x16", [P, IT, XW], F16)
        wt_s = sb("wt_s", [P, F], F32)
        bias_s = sb("bias_s", [P, F], F32)
        w_s = sb("w_s", [F, F], F32)
        a_s = sb("a_s", [F, 2], F32)
        a_bc = sb("a_bc", [F, 2, P], F32)
        x_all = off[:, 0:2 * TILES * F].bitcast(F32).rearrange("p (t f) -> p t f", f=F)
        e_all = off[:, 2 * TILES * F:4 * TILES * F].bitcast(F32).rearrange("p (t f) -> p t f", f=F)
        tmp = off[:, 4 * TILES * F:6 * TILES * F].bitcast(F32).rearrange("p (t f) -> p t f", f=F)
        EW = OCT * IB
        slot2 = [(OCTS - RING + v // 2) % RING for v in range(OPB)]
        edge2 = [off[:, slot2[v] * EW + v % 2 * (EW // 2):slot2[v] * EW + (v % 2 + 1) * (EW // 2)].bitcast(FP8)
                 for v in range(OPB)]
        x16_all = adjb[:, 0:3, :].rearrange("p a b -> p (a b)")[:, 0:TILES * XW // 2].bitcast(F16)\
            .rearrange("p (b t w) -> p b t w", b=BLOCKS, t=IT)
        bestf = cand[:, :].bitcast(F32)
        agg = ent[:, 0:18, :].rearrange("p a b -> p (a b)")[:, 0:9 * XU].rearrange("p (t w) -> p t w", t=9)
        nx = prob[:, 0, :].rearrange("p (t w) -> p t w", t=IT)
        nxT = prob[:, 1, :]

        ps = ctx.enter_context(nc.psum_tensor("ps", [P, 8, HALF], F32))
        score = [ps[:, 2 * n:2 * n + 2, :].rearrange("p a b -> p (a b)") for n in range(2)]
        sums = ps[0:FE, 4:6, :].rearrange("p a b -> p (a b)")
        turn = ps[:, 6:8, :].rearrange("p a (t w) -> p (a t) w", w=P)
        turn16 = ps[0:3 * IT, 6, 0:HALF].bitcast(BF16)[:, 0:P]
        agg_ps = [ps[:, 3 * n:3 * n + 3, 0:3 * XU] for n in range(2)]

        ld_in = sem("ld_in")
        ld_x = sem("ld_x")
        ld_w = sem("ld_w")
        prep = sem("prep")
        pe_prep = sem("pe_prep")
        const_in = sem("const_in")
        srow_out = sem("srow_out")
        srow_tile = sem("srow_tile")
        pool_c = sem("pool_c")
        range_in = sem("range_in")
        range_out = sem("range_out")
        sbc_ld = sem("sbc_ld")
        adj_ld = [sem(f"adj_ld{k}") for k in range(PAIRS)]
        edge_st = [sem(f"edge_st{k}") for k in range(PAIRS)]
        off_in = sem("off_in")
        cand_in = sem("cand_in")
        best_up = sem("best_up")
        best_clear = sem("best_clear")
        pair_done = sem("pair_done")
        oct_done = sem("oct_done")
        stat_step = sem("stat_step")
        epi_step = sem("epi_step")
        fin_step = sem("fin_step")
        epi_a = sem("epi_a")
        epi_b = sem("epi_b")
        best_in = sem("best_in")
        best_T = sem("best_T")
        parts_in = sem("parts_in")
        parts_T = sem("parts_T")
        partT_in = sem("partT_in")
        rows_ld = sem("rows_ld")
        rows_due = sem("rows_due")
        shift_in = sem("shift_in")
        decay_in = sem("decay_in")
        relu_in = sem("relu_in")
        relu_due = sem("relu_due")
        score_in = sem("score_in")
        prob_in = sem("prob_in")
        acc_in = sem("acc_in")
        acc_T = sem("acc_T")
        xblk_ld = sem("xblk_ld")
        elu_in = sem("elu_in")
        elu_out = sem("elu_out")
        var_in = sem("var_in")
        var_out = sem("var_out")
        x16_in = sem("x16_in")
        x16_st = sem("x16_st")
        x1_st = sem("x1_st")
        x1_free = sem("x1_free")
        e2_ld = [sem(f"e2_ld{v}") for v in range(OPB)]
        x2_ld = [sem(f"x2_ld{b}") for b in range(BLOCKS)]
        e2_used = sem("e2_used")
        e2_seen = sem("e2_seen")
        agg_free = sem("agg_free")
        nx_ld = sem("nx_ld")
        nx_in = sem("nx_in")
        nx_x_in = sem("nx_x_in")
        nx_T = sem("nx_T")
        nxT_in = sem("nxT_in")
        y_ps = sem("y_ps")
        out_in = sem("out_in")
        out_st = sem("out_st")


        block = ctx.enter_context(nc.Block())

        def whole(ap):
            return ap.rearrange("a p n -> (a p) n")

        def over_f(ap):
            return ap.unsqueeze(2).to_broadcast([P, IT, F])

        def over_t(ap):
            return ap.unsqueeze(1).to_broadcast([P, IT, F])

        def pair_of(o, k):
            return off[:, bass.ds((o % RING) * (OCT * IB) + k * PW, PW)]

        def edge_load(sp, b, v):
            sp.dma_start(edge2[v].bitcast(I16).rearrange("p (k n) -> p k n", k=PAIRS),
                         edges[bass.ds(b * (OPB * PAIRS) + v * PAIRS, PAIRS)]
                         .rearrange("k p n -> p k n")).then_inc(e2_ld[v], 16)

        @block.sync
        def _(sp):
            sp.dma_start(e_all, ent_t.rearrange("p (t f) -> p t f", f=F)).then_inc(ld_in, 16)
            sp.dma_start(w_s[:], w_t).then_inc(ld_in, 16)
            sp.dma_start(a_s[:], a_col).then_inc(ld_in, 16)
            sp.dma_start(x_all, x_t.rearrange("p (t f) -> p t f", f=F)).then_inc(ld_x, 16)
            for k in range(PAIRS):
                sp.dma_start(adjb[:, k, :], adj_t[k]).then_inc(adj_ld[k], 16)
            sp.dma_start(wt_s[:], wt1).then_inc(ld_w, 16)
            sp.dma_start(bias_s[:], bias1.to_broadcast([P, F])).then_inc(ld_w, 16)
            sp.wait_ge(srow_tile, 1)
            sp.dma_start(s_row, s_rows[:, :]).then_inc(srow_out, 16)
            with sp.Fori(0, OCTS - 1) as o:
                for k in range(PAIRS):
                    sp.wait_ge(pair_done, o * PAIRS + (k + 1))
                    sp.dma_start(adjb[:, k, :], whole(adj_t[bass.ds(o * PAIRS + (k + PAIRS), 1)]))\
                      .then_inc(adj_ld[k], 16)
                    sp.dma_start(whole(edges[bass.ds(o * PAIRS + k, 1)]), edge[:, k, :].bitcast(I16))\
                      .then_inc(edge_st[k], 16)
            for k in range(PAIRS):
                sp.wait_ge(pair_done, (OCTS - 1) * PAIRS + k + 1)
                sp.dma_start(edges[(OCTS - 1) * PAIRS + k], edge[:, k, :].bitcast(I16)).then_inc(edge_st[k], 16)
            for b in range(BLOCKS):
                if b == BLOCKS - 1:
                    for k in range(PAIRS):
                        sp.wait_ge(edge_st[k], 16 * OCTS)
                    for v in range(OPB):
                        sp.wait_ge(oct_done, OCTS - RING + v // 2 + 1)
                        edge_load(sp, 0, v)
                sp.wait_ge(x16_st, 16 * (b + 1))
                sp.dma_start(x16_all[:, b], x16_d[b].rearrange("p (t w) -> p t w", t=IT)).then_inc(x2_ld[b], 16)
            with sp.Fori(1, BLOCKS) as b:
                for v in range(OPB):
                    sp.wait_ge(e2_used, (b - 1) * OPB + (v + 1))
                    edge_load(sp, b, v)

        @block.gpsimd
        def _(pool):
            pool.memset(ident[:], 0.0).then_inc(pool_c, 1)
            pool.memset(half[:], -0.5).then_inc(pool_c, 1)
            pool.wait_ge(pool_c, 2)
            pool.affine_select(out=ident[:], in_=ident[:], compare_op=ALU.not_equal, fill=1.0, base=0,
                               pattern=[[-1, P]], channel_multiplier=1).then_inc(pool_c, 1)
            pool.wait_ge(range_in, 2)
            pool.partition_all_reduce(small[:, 2:4], small[:, 0:2], P, RMAX).then_inc(range_out, 1)

            def load_s(b):
                pool.dma_start(s_bc[:, bass.ds((b % 2) * IB, IB)],
                               s_row.rearrange("(b t) p -> b (t p)", b=BLOCKS)[bass.ds(b, 1), :]
                               .to_broadcast([P, IB])).then_inc(sbc_ld, 16)

            def load_rows(b, c):
                pool.wait_ge(partT_in, 2 * b + c + 1)
                pool.sem_inc(rows_due, 1)
                pool.dma_start(rows[:, c, :].rearrange("k (t p) -> k t p", p=P), partT[:, :])\
                    .then_inc(rows_ld, 16)

            def load_x(b):
                pool.dma_start(xblk[:].rearrange("p t f -> p (t f)"),
                               x_t.rearrange("p (b n) -> b p n", b=BLOCKS)[bass.ds(b, 1)]
                               .rearrange("a p n -> (a p) n")).then_inc(xblk_ld, 16)

            def finish_x1(b):
                pool.wait_ge(var_in, b + 1)
                pool.tensor_tensor(mom[:, 7, :], mom[:, 6, :], half[:, :], ALU.pow).then_inc(var_out, 1)
                pool.wait_ge(x16_in, b + 1)
                pool.dma_start(whole(x16_d[bass.ds(b, 1)]),
                               x16[:, :, :].rearrange("p t w -> p (t w)")).then_inc(x16_st, 16)
                pool.dma_start(whole(x1_d[bass.ds(b, 1)]),
                               ya[:, :, :].rearrange("p t f -> p (t f)")).then_inc(x1_st, 16)
                pool.wait_ge(x16_st, b * 16 + 16)
                pool.wait_ge(x1_st, b * 16 + 16)
                pool.sem_inc(x1_free, 1)

            pool.sem_inc(x1_free, 1)
            pool.wait_ge(srow_out, 16)
            load_s(0)
            pool.wait_ge(sbc_ld, 16)
            load_s(1)
            load_x(0)
            load_rows(0, 0)
            load_rows(0, 1)

            def block_of(b, more):
                load_rows(b, 0)
                if more:
                    pool.wait_ge(sbc_ld, b * 16 + 16)
                    pool.wait_ge(oct_done, b * OPB)
                    load_s(b + 1)
                load_rows(b, 1)
                finish_x1(b - 1)
                load_x(b)

            with pool.Fori(1, BLOCKS - 1) as b:
                block_of(b, True)
            block_of(BLOCKS - 1, False)
            finish_x1(BLOCKS - 1)
            pool.wait_ge(x1_st, 16 * BLOCKS)
            with pool.Fori(0, BLOCKS) as b:
                pool.wait_ge(var_in, b + (BLOCKS + 1))
                pool.tensor_tensor(mom[:, 7, :], mom[:, 6, :], half[:, :], ALU.pow).then_inc(var_out, 1)

        @block.vector
        def _(dve):
            V = nc.vector
            at = [0]

            def link(ins, sem_, base=0):
                at[0] += 1
                ins.then_inc(sem_, 1)
                dve.wait_ge(sem_, base + at[0])

            V.memset(a_bc[:].rearrange("p a b -> p (a b)"), 1.0).then_inc(prep, 1)
            V.memset(onesr[:], 1.0).then_inc(prep, 1)
            V.memset(ones[:], 1.0).then_inc(prep, 1)
            V.memset(ent[:, :, F:FE], 1.0).then_inc(prep, 1)
            V.memset(x16[:, :, 2 * F:2 * F + 1], 1.0).then_inc(prep, 1)
            V.memset(x16[:, :, 2 * F + 1:XW], 0.0).then_inc(prep, 1)
            at[0] = 6
            dve.wait_ge(pool_c, 3)
            V.tensor_scalar(negbig[:], ident[:], -BIG, None, ALU.mult).then_inc(prep, 1)
            V.tensor_copy(ident16[:], ident[:]).then_inc(prep, 1)
            at[0] = 8
            dve.wait_ge(prep, 8)
            dve.wait_ge(ld_in, 48)
            for k in range(2):
                link(V.tensor_scalar(a_bc[:, k, :], a_bc[:, k, :], a_s[:, k:k + 1], None, ALU.mult), prep)
            V.tensor_copy(ent[:, :, 0:F], e_all).then_inc(const_in, 1)
            dve.wait_ge(pe_prep, 1)
            link(V.tensor_copy(wa[:], ps[:, 6, 0:2 * F].rearrange("p (k f) -> p k f", k=2)), prep)

            def over_tiles(ap):
                return ap.unsqueeze(1).to_broadcast([P, TILES, F])

            link(V.tensor_tensor(tmp, e_all, over_tiles(wa[:, 1, :]), ALU.mult), prep)
            link(V.tensor_reduce(t_lo[:], tmp, AX.X, ALU.add), prep)
            V.tensor_reduce(small[:, 0:1], t_lo[:], AX.X, ALU.max).then_inc(range_in, 1)
            link(V.tensor_reduce(small[:, 8:9], t_lo[:], AX.X, ALU.min), prep)
            V.tensor_scalar(small[:, 1:2], small[:, 8:9], -1.0, None, ALU.mult).then_inc(range_in, 1)
            dve.wait_ge(ld_x, 16)
            link(V.tensor_tensor(tmp, x_all, over_tiles(wa[:, 0, :]), ALU.mult), prep)
            link(V.tensor_reduce(s_col[:], tmp, AX.X, ALU.add), prep)
            V.tensor_reduce(mean_e[:], e_all.rearrange("p t f -> p f t"), AX.X, ALU.add).then_inc(const_in, 1)
            dve.wait_ge(pe_prep, 2)
            V.tensor_copy(s_rows[:, :], ps[0:TILES, 7, 0:P]).then_inc(srow_tile, 1)
            dve.wait_ge(range_out, 1)
            link(V.tensor_tensor(small[:, 4:5], small[:, 2:3], small[:, 3:4], ALU.add), prep)
            link(V.tensor_scalar(small[:, 5:6], small[:, 4:5], 1.0 / CODES, 1e-30, ALU.mult, ALU.max), prep)
            link(V.reciprocal(small[:, 6:7], small[:, 5:6]), prep)
            link(V.tensor_tensor(small[:, 9:10], small[:, 3:4], small[:, 5:6], ALU.add), prep)
            link(V.tensor_scalar(small[:, 7:8], small[:, 9:10], -1.0, None, ALU.mult), prep)
            link(V.tensor_scalar(code[:], t_lo[:], small[:, 3:4], small[:, 6:7], ALU.add, ALU.mult), prep)
            link(V.tensor_scalar(code[:], code[:], 2.0, None, ALU.add), prep)
            link(V.tensor_scalar(t_hi[:], t_lo[:], REST, None, ALU.mult), prep)
            V.tensor_scalar(t_lo[:], t_lo[:], SLOPE, None, ALU.mult).then_inc(const_in, 1)
            dve.wait_ge(pe_prep, 3)
            link(V.tensor_scalar(mean_e[:], ps[:, 6, 2 * F:3 * F], 1.0 / N, None, ALU.mult), prep)

            def sweep_a(o, c, oo, ring_free=True, first=False):
                for k in range(PAIRS):
                    if ring_free:
                        dve.wait_ge(score_in, (o - RING) * OCT + (k + 1) * PAIR)
                    if not first:
                        dve.wait_ge(edge_st[k], o * 16)
                    dve.wait_ge(adj_ld[k], o * 16 + 16)
                    pair = pair_of(o, k)
                    V.tensor_scalar(pair, adjb[:, k, :], 0.0, None, ALU.is_le).then_inc(off_in, 1)
                    V.tensor_scalar(edge[:, k, :], adjb[:, k, :], 1.0, None, ALU.is_equal,
                                    saturate=False).then_inc(pair_done, 1)
                    dve.wait_ge(off_in, o * PAIRS + (k + 1))
                    if not first or k:
                        dve.wait_ge(best_up, o * PAIRS + k)
                    for n in range(PAIR):
                        tile_off = off[:, bass.ds((o % RING) * (OCT * IB) + (k * PAIR + n) * IB, IB)]
                        jt = (c * OPU + oo) * OCT + (k * PAIR + n)
                        V.tensor_scalar(cand[:, n * IB:(n + 1) * IB], tile_off, 0.0,
                                        code[:, bass.ds(jt, 1)], ALU.is_equal, ALU.mult).then_inc(cand_in, 1)
                    dve.wait_ge(cand_in, o * OCT + (k + 1) * PAIR)
                    V.tensor_tensor(best[:], best[:], cand[:], ALU.max).then_inc(best_up, 1)

            STATS = 8

            def stats(b, c):
                u = 2 * b + c
                at[0] = 0

                def step(ins):
                    link(ins, stat_step, u * STATS)

                dve.wait_ge(best_up, (u + 1) * (OPU * PAIRS))
                V.tensor_tensor(bestf, best[:, 0:IB], best[:, IB:PW], ALU.max).then_inc(best_in, 1)
                dve.wait_ge(best_T, u + 1)
                step(V.tensor_reduce(stat[:, 0, :], turn, AX.X, ALU.max))
                step(V.tensor_scalar(stat[:, 1, :], stat[:, 0, :], small[:, 5:6], small[:, 7:8],
                                     ALU.mult, ALU.add))
                s_b = s_col[:, bass.ds(b * IT, IT)]
                step(V.tensor_tensor(stat[:, 2, :], stat[:, 1, :], s_b, ALU.add))
                step(V.scalar_tensor_tensor(maxes[:, c, :], stat[:, 2, :], SLOPE, stat[:, 2, :],
                                            ALU.mult, ALU.max))
                step(V.scalar_tensor_tensor(stat[:, 3, :], s_b, SLOPE, maxes[:, c, :],
                                            ALU.mult, ALU.subtract))
                step(V.tensor_copy(parts[:, 0, :], stat[:, 3, :]))
                step(V.tensor_tensor(stat[:, 4, :], stat[:, 3, :], parts[:, 0, :], ALU.subtract))
                step(V.tensor_copy(parts[:, 1, :], stat[:, 4, :]))
                V.tensor_tensor(parts[:, 2, :], stat[:, 4, :], parts[:, 1, :], ALU.subtract).then_inc(parts_in, 1)
                if c == 1:
                    V.tensor_tensor(shift[:], maxes[:, 0, :], maxes[:, 1, :], ALU.subtract).then_inc(shift_in, 1)
                dve.wait_ge(parts_T, u + 1)
                if not (isinstance(u, int) and u == 0):
                    dve.wait_ge(rows_ld, u * 16)
                V.tensor_copy(partT[:, :], turn16).then_inc(partT_in, 1)
                assert at[0] == STATS

            def evac0(b):
                dve.wait_ge(acc_T, 2 * b + 2)
                V.tensor_copy(acc0[:, :, :], turn[:, :, 0:FE]).then_inc(epi_a, 1)

            EPI = 16

            def evac1(b):
                at[0] = 0

                def step(ins):
                    link(ins, epi_step, b * EPI)

                dve.wait_ge(epi_a, b + 1)
                dve.wait_ge(decay_in, b + 1)
                step(V.tensor_tensor(acc0[:, :, :], acc0[:, :, :],
                                     decay[:, :].unsqueeze(2).to_broadcast([P, IT, FE]), ALU.mult))
                dve.wait_ge(acc_T, 2 * b + 3)
                step(V.tensor_tensor(acc0[:, :, :], turn[:, :, 0:FE], acc0[:, :, :], ALU.add))
                den = acc0[:, :, F:FE].rearrange("p t o -> p (t o)")
                step(V.tensor_scalar(mom[:, 0, :], den, 0.0, None, ALU.is_equal))
                step(V.tensor_tensor(mom[:, 1, :], den, mom[:, 0, :], ALU.add))
                step(V.reciprocal(mom[:, 2, :], mom[:, 1, :]))
                dve.wait_ge(x1_free, b + 1)
                step(V.tensor_tensor(ya[:], acc0[:, :, 0:F], over_f(mom[:, 2, :]), ALU.mult))
                step(V.tensor_tensor(yb[:], over_t(mean_e[:]), over_f(mom[:, 0, :]), ALU.mult))
                step(V.tensor_tensor(ya[:], ya[:], yb[:], ALU.add))
                dve.wait_ge(xblk_ld, b * 16 + 16)
                step(V.tensor_tensor(ya[:], ya[:], xblk[:], ALU.add))
                V.tensor_scalar(yb[:], ya[:], 0.0, None, ALU.min).then_inc(elu_in, 1)

            def norm(step, b):
                step(V.tensor_reduce(mom[:, 3, :], ya[:], AX.X, ALU.add))
                step(V.tensor_scalar(mom[:, 4, :], mom[:, 3, :], 1.0 / F, None, ALU.mult))
                step(V.tensor_tensor(ya[:], ya[:], over_f(mom[:, 4, :]), ALU.subtract))
                step(V.tensor_tensor(yb[:], ya[:], ya[:], ALU.mult))
                step(V.tensor_reduce(mom[:, 5, :], yb[:], AX.X, ALU.add))
                V.tensor_scalar(mom[:, 6, :], mom[:, 5, :], 1.0 / F, EPS, ALU.mult, ALU.add).then_inc(var_in, 1)
                dve.wait_ge(var_out, b + 1)

            def layer0_end(b):
                at[0] = 9

                def step(ins):
                    link(ins, epi_step, b * EPI)

                dve.wait_ge(elu_out, b + 1)
                step(V.scalar_tensor_tensor(ya[:], ya[:], 0.0, yb[:], ALU.max, ALU.add))
                step(V.scalar_tensor_tensor(ya[:], ya[:], -1.0, xblk[:], ALU.add, ALU.add))
                norm(step, b)
                V.tensor_tensor(ya[:], ya[:], over_f(mom[:, 7, :]), ALU.mult).then_inc(epi_b, 1)
                dve.wait_ge(epi_b, b * 3 + 1)
                V.tensor_copy(x16[:, :, 0:F], ya[:]).then_inc(epi_b, 1)
                dve.wait_ge(epi_b, b * 3 + 2)
                V.tensor_tensor(yb[:], ya[:], x16[:, :, 0:F], ALU.subtract).then_inc(epi_b, 1)
                dve.wait_ge(epi_b, b * 3 + 3)
                V.tensor_scalar(x16[:, :, F:2 * F], yb[:], LO, None, ALU.mult).then_inc(x16_in, 1)
                assert at[0] == EPI

            def clear_best(b):
                V.memset(best[:].bitcast(I32), 0).then_inc(best_clear, 1)
                dve.wait_ge(best_clear, b + 1)

            clear_best(0)
            sweep_a(0, 0, 0, False, True)
            with dve.Fori(1, OPU) as oo:
                sweep_a(oo, 0, oo, False)
            stats(0, 0)
            for oo in range(OPU):
                sweep_a(OPU + oo, 1, oo, OPU + oo >= RING)
            stats(0, 1)
            clear_best(1)

            def block_of(b):
                with dve.Fori(0, 2) as oo:
                    sweep_a(b * OPB + oo, 0, oo, True)
                evac0(b - 1)
                with dve.Fori(2, OPU) as oo:
                    sweep_a(b * OPB + oo, 0, oo, True)
                dve.wait_ge(epi_a, b)
                stats(b, 0)
                with dve.Fori(0, 2) as oo:
                    sweep_a(b * OPB + OPU + oo, 1, oo, True)
                evac1(b - 1)
                with dve.Fori(2, OPU) as oo:
                    sweep_a(b * OPB + OPU + oo, 1, oo, True)
                stats(b, 1)
                clear_best(b + 1)
                layer0_end(b - 1)

            with dve.Fori(1, BLOCKS) as b:
                block_of(b)
            last = BLOCKS - 1
            evac0(last)
            dve.wait_ge(prob_in, BLOCKS * TILES + FREE)
            V.memset(agg_ps[0], 0.0).then_inc(agg_free, 1)
            dve.wait_ge(acc_in, 2 * BLOCKS)
            V.memset(agg_ps[1], 0.0).then_inc(agg_free, 1)
            evac1(last)
            layer0_end(last)

            FIN = 10

            def layer1_end(b, n, first=False):
                at[0] = 0

                def step(ins):
                    link(ins, fin_step, b * FIN)

                dve.wait_ge(e2_used, (b + 1) * OPB)
                step(V.tensor_copy(agg.rearrange("p (a t) w -> p a (t w)", a=3), agg_ps[n]))
                V.memset(agg_ps[n], 0.0).then_inc(agg_free, 1)
                step(V.reciprocal(mom[:, 0, :], agg[:, 0:IT, 2 * F:XU].rearrange("p t o -> p (t o)")))
                if first:
                    dve.wait_ge(x1_st, 16 * BLOCKS)
                else:
                    dve.wait_ge(out_st, b * 16)
                step(V.scalar_tensor_tensor(ya[:], agg[:, 0:IT, F:2 * F], 1.0 / LO, agg[:, 0:IT, 0:F],
                                            ALU.mult, ALU.add))
                V.tensor_tensor(nx[:, :, 0:F], ya[:], over_f(mom[:, 0, :]), ALU.mult).then_inc(nx_in, 1)
                dve.wait_ge(y_ps, b + 1)
                step(V.tensor_tensor(ya[:], ps[:, 6, :].rearrange("p (t f) -> p t f", f=F), xblk[:], ALU.add))
                step(V.tensor_tensor(ya[:], ya[:], over_t(bias_s[:]), ALU.add))
                norm(step, b + BLOCKS)
                V.tensor_tensor(ya[:], ya[:], over_f(mom[:, 7, :]), ALU.mult).then_inc(out_in, 1)
                assert at[0] == FIN

            dve.wait_ge(ld_w, 32)
            layer1_end(0, 0, True)
            layer1_end(1, 1)
            with dve.Fori(1, BLOCKS // 2) as two:
                for n in range(2):
                    layer1_end(two * 2 + n, n)

        @block.scalar
        def _(act):
            A = nc.scalar

            def relu(b, c, oo, t):
                act.wait_ge(prob_in, (b * OPB + (c * OPU + oo)) * OCT + (t + 1))
                if isinstance(oo, int):
                    act.sem_inc(relu_due, 1)
                jt = (c * OPU + oo) * OCT + t
                A.activation(score[t % 2], s_bc[:, bass.ds((b % 2) * IB, IB)], ACT.Relu, scale=REST,
                             bias=t_hi[:, bass.ds(jt, 1)]).then_inc(relu_in, 1)

            def octet(b, c, oo, after, then):
                for t in range(OCT):
                    act.wait_ge(score_in, (b * OPB + (c * OPU + oo)) * OCT + (t + 1))
                    jt = (c * OPU + oo) * OCT + t
                    A.activation(prob[:, t % 2, :], score[t % 2], ACT.Exp,
                                 bias=t_lo[:, bass.ds(jt, 1)]).then_inc(prob_in, 1)
                    if t in then:
                        then[t]()
                    if t + 2 < OCT:
                        relu(b, c, oo, t + 2)
                    elif after:
                        if t + 2 == OCT and after[1] == 0 and c == 1:
                            act.wait_ge(sbc_ld, after[0] * 16 + 16)
                        relu(*after, t + 2 - OCT)

            def evac(u):
                act.wait_ge(oct_done, u * OPU + OPU)
                act.wait_ge(acc_T, u + 1)
                A.copy(accT[:, :], sums).then_inc(acc_in, 1)

            def exp_decay(b):
                act.wait_ge(shift_in, b + 1)
                A.activation(decay[:], shift[:], ACT.Exp).then_inc(decay_in, 1)

            def exp_elu(b):
                act.wait_ge(elu_in, b + 1)
                A.activation(yb[:], yb[:], ACT.Exp).then_inc(elu_out, 1)

            def unit(b, c, after):
                u = 2 * b + c
                if isinstance(u, int) and u == 0:
                    octet(b, c, 0, (b, c, 1), {})
                else:
                    octet(b, c, 0, (b, c, 1), {0: lambda: evac(u - 1)})
                with act.Fori(1, OPU - 1) as oo:
                    octet(b, c, oo, (b, c, oo + 1), {})
                if c == 1:
                    octet(b, c, OPU - 1, after, {0: lambda: exp_decay(b)})
                elif isinstance(b, int) and b == 0:
                    octet(b, c, OPU - 1, after, {})
                else:
                    octet(b, c, OPU - 1, after, {0: lambda: exp_elu(b - 1)})

            act.sem_inc(prob_in, FREE)
            act.wait_ge(const_in, 3)
            act.wait_ge(pe_prep, 4)
            act.wait_ge(sbc_ld, 16)
            last = BLOCKS - 1
            relu(0, 0, 0, 0)
            relu(0, 0, 0, 1)
            unit(0, 0, (0, 1, 0))
            with act.Fori(0, last) as b:
                unit(b, 1, (b + 1, 0, 0))
                unit(b + 1, 0, (b + 1, 1, 0))
            unit(last, 1, None)
            evac(2 * last + 1)
            exp_elu(last)
            def layer1(b, first=False):
                if not first:
                    act.wait_ge(out_in, b)
                    act.dma_start(whole(out[bass.ds(b - 1, 1)]), ya[:].rearrange("p t f -> p (t f)"))\
                        .then_inc(out_st, 16)
                act.dma_start(xblk[:].rearrange("p t f -> p (t f)"), whole(x1_d[bass.ds(b, 1)]))\
                    .then_inc(nx_ld, 16)
                act.wait_ge(nx_ld, b * 16 + 16)
                A.copy(nx[:, :, F:2 * F], xblk[:]).then_inc(nx_x_in, 1)
                act.wait_ge(nx_T, b + 1)
                A.copy(nxT, turn.rearrange("p t w -> p (t w)")).then_inc(nxT_in, 1)

            act.wait_ge(x1_st, 16 * BLOCKS)
            layer1(0, True)
            with act.Fori(1, BLOCKS) as b:
                layer1(b)
            act.wait_ge(out_in, BLOCKS)
            act.dma_start(out[BLOCKS - 1], ya[:].rearrange("p t f -> p (t f)")).then_inc(out_st, 16)
            act.wait_ge(out_st, 16 * BLOCKS)

        @block.tensor
        def _(pe):
            M = nc.tensor.matmul
            pe.wait_ge(prep, 10)
            for k in range(2):
                ins = M(ps[:, 6, k * F:(k + 1) * F], a_bc[:, k, :], w_s[:, :], start=True, stop=True)
            ins.then_inc(pe_prep, 1)
            pe.wait_ge(prep, 16)
            nc.tensor.transpose(ps[0:TILES, 7, 0:P], s_col[:, :], ident[:, :]).then_inc(pe_prep, 1)
            pe.wait_ge(const_in, 2)
            M(ps[:, 6, 2 * F:3 * F], ones[:, :], mean_e[:, :], start=True, stop=True).then_inc(pe_prep, 1)
            for n in range(2):
                for h in range(2):
                    for q in range(HALF // P):
                        at = h * HALF + q * P
                        ins = M(score[n][:, at:at + P], ident16[:, :], negbig[:, :], start=q == 0, stop=True,
                                skip_group_check=True)
            ins.then_inc(pe_prep, 1)

            def turn_best(u):
                pe.wait_ge(best_in, u + 1)
                for t in range(IT):
                    ins = nc.tensor.transpose(turn[:, t, :], bestf[:, t * P:(t + 1) * P], ident[:, :])
                ins.then_inc(best_T, 1)

            def turn_parts(u):
                pe.wait_ge(parts_in, u + 1)
                nc.tensor.transpose(turn16, parts[:, :, :].rearrange("p k t -> p (k t)"),
                                    ident16[:, :]).then_inc(parts_T, 1)

            def turn_sums(u):
                pe.wait_ge(acc_in, u + 1)
                for t in range(IT):
                    ins = nc.tensor.transpose(turn[:, t, 0:FE], accT[:, t * P:(t + 1) * P], ident[0:FE, 0:FE])
                ins.then_inc(acc_T, 1)

            def add(b, c, oo, t):
                o = b * OPB + (c * OPU + oo)
                pe.wait_ge(relu_in, o * OCT + (t + 1))
                for h in range(2):
                    M(score[t % 2][:, h * HALF:(h + 1) * HALF], negbig[:, :],
                      off[:, bass.ds((o % RING) * (OCT * IB) + t * IB + h * HALF, HALF)],
                      start=False, stop=True, skip_group_check=True)
                for h in range(2):
                    ins = M(score[t % 2][:, h * HALF:(h + 1) * HALF], onesr[:, :],
                            rows[:, c, h * HALF:(h + 1) * HALF], start=False, stop=True,
                            skip_group_check=True)
                ins.then_inc(score_in, 1)

            def octet(b, c, oo, after, then, fresh=False):
                o = b * OPB + (c * OPU + oo)
                for t in range(OCT):
                    if t + 1 < OCT:
                        add(b, c, oo, t + 1)
                    elif after:
                        if oo is last_oo:
                            pe.wait_ge(rows_ld, (2 * b + c) * 16 + 32)
                        add(*after, 0)
                    if fresh and t == 0 and not (isinstance(b, int) and 2 * b + c == 0):
                        pe.wait_ge(acc_in, 2 * b + c)
                    pe.wait_ge(prob_in, o * OCT + (t + 1 + FREE))
                    jt = (c * OPU + oo) * OCT + t
                    for h in range(2):
                        ins = M(sums[:, h * HALF:(h + 1) * HALF],
                                ent[:, jt, :], prob[:, t % 2, h * HALF:(h + 1) * HALF],
                                start=fresh and t == 0, stop=True, skip_group_check=True)
                    if t == OCT - 1:
                        ins.then_inc(oct_done, 1)
                    if t in then:
                        then[t]()

            last_oo = OPU - 1

            def unit(b, c, after):
                u = 2 * b + c
                first = isinstance(u, int) and u == 0
                octet(b, c, 0, (b, c, 1), {} if first else {3: lambda: turn_sums(u - 1)}, fresh=True)
                for oo in range(1, OPU - 1):
                    octet(b, c, oo, (b, c, oo + 1), {})
                octet(b, c, last_oo, after, {0: lambda: turn_best(u + 1), 4: lambda: turn_parts(u + 1)} if after else {})

            pe.sem_inc(acc_T, 1)
            turn_best(0)
            turn_parts(0)
            last = BLOCKS - 1
            for n in range(12):
                M(turn[:, 4:8, :].rearrange("p t w -> p (t w)"), negbig[:, :], off[:, 0:HALF],
                  start=True, stop=True, skip_group_check=True)
            pe.wait_ge(rows_ld, 16)
            add(0, 0, 0, 0)
            unit(0, 0, (0, 1, 0))
            with pe.Fori(0, last) as b:
                unit(b, 1, (b + 1, 0, 0))
                unit(b + 1, 0, (b + 1, 1, 0))
            unit(last, 1, None)
            pe.wait_ge(epi_a, BLOCKS)
            turn_sums(2 * last + 1)

            def edges_of(b, n, then, first=False):
                pe.wait_ge(agg_free, b + 1)
                for v in range(OPB):
                    pe.wait_ge(e2_ld[v], b * 16 + 16)
                    pe.sem_inc(e2_seen, 1)
                    if first:
                        pe.wait_ge(x2_ld[v], 16)
                    for t in range(OCT):
                        for m in range(IT):
                            ins = M(agg_ps[n][:, m // 3, (m % 3) * XU:(m % 3 + 1) * XU],
                                    edge2[v][:, t * IB + m * P:t * IB + (m + 1) * P],
                                    x16_all[:, v, t, 0:XU], start=False, stop=True, skip_group_check=True)
                    ins.then_inc(e2_used, 1)
                    if v in then:
                        then[v]()

            def turn_nx(b):
                pe.wait_ge(nx_in, b + 1)
                pe.wait_ge(nx_x_in, b + 1)
                for m in range(IT):
                    ins = nc.tensor.transpose(turn[:, m, :], nx[:, m, :], ident[:, :])
                ins.then_inc(nx_T, 1)

            def apply_weight(b):
                pe.wait_ge(nxT_in, b + 1)
                for m in range(IT):
                    ins = M(ps[:, 6, m * F:(m + 1) * F], nxT[:, m * P:(m + 1) * P], wt_s[:, :],
                            start=True, stop=True)
                ins.then_inc(y_ps, 1)

            def behind(b):
                return {3: lambda: turn_nx(b), 5: lambda: apply_weight(b)}

            edges_of(0, 0, {}, True)
            with pe.Fori(0, BLOCKS // 2 - 1) as two:
                edges_of(two * 2 + 1, 1, behind(two * 2))
                edges_of(two * 2 + 2, 0, behind(two * 2 + 1))
            edges_of(BLOCKS - 1, 1, behind(BLOCKS - 2))
            turn_nx(BLOCKS - 1)
            apply_weight(BLOCKS - 1)


def kernel(x, adj, L0_gnn_entity_embs, L0_gnn_W, L0_gnn_a, L1_gnn_weight, L1_gnn_bias):
    import numpy as np
    import concourse.bacc as bacc
    from concourse.bass_utils import run_bass_kernel_spmd

    def tiled(a):
        return np.ascontiguousarray(np.asarray(a).reshape(TILES, P, F).transpose(1, 0, 2)).reshape(P, TILES * F)

    adj_t = np.asarray(adj).reshape(BLOCKS, IB, OPB, PAIRS, PAIR, P).transpose(0, 2, 3, 5, 4, 1)
    arrays = {
        "x_t": tiled(x),
        "adj_t": np.ascontiguousarray(adj_t).reshape(OCTS * PAIRS, P, PW),
        "ent_t": tiled(L0_gnn_entity_embs),
        "w_t": np.ascontiguousarray(np.asarray(L0_gnn_W).T),
        "a_col": np.ascontiguousarray(np.asarray(L0_gnn_a).reshape(2, F).T),
        "wt1": np.ascontiguousarray(np.asarray(L1_gnn_weight)),
        "bias1": np.ascontiguousarray(np.asarray(L1_gnn_bias).reshape(1, F)),
    }
    nc = bacc.Bacc("TRN2", target_bir_lowering=False, num_devices=1)
    args = [nc.dram_tensor(k, a.shape, mybir.dt.from_np(a.dtype), kind="ExternalInput").ap()
            for k, a in arrays.items()]
    out = nc.dram_tensor("out", (BLOCKS, P, IT * F), F32, kind="ExternalOutput").ap()
    gnn_program(nc, *args, out)
    got = run_bass_kernel_spmd(nc, [arrays], core_ids=[0]).results[0]["out"]
    return np.ascontiguousarray(np.asarray(got).reshape(BLOCKS, P, IT, F).transpose(0, 2, 1, 3)).reshape(N, F)
```

```python
from contextlib import ExitStack

import concourse.bass as bass
from concourse import mybir

F32 = mybir.dt.float32
BF16 = mybir.dt.bfloat16
F16 = mybir.dt.float16
I16 = mybir.dt.int16
I32 = mybir.dt.int32
FP8 = mybir.dt.float8e4
ALU = mybir.AluOpType
ACT = mybir.ActivationFunctionType
AX = mybir.AxisListType
RMAX = bass.bass_isa.ReduceOp.max

P = 128
N = 8192
F = 64
TILES = N // P
IB = 1024
BLOCKS = N // IB
IT = IB // P
PAIR = 2
PAIRS = 4
OCT = PAIR * PAIRS
UNIT = 32
OPU = UNIT // OCT
OPB = TILES // OCT
OCTS = BLOCKS * OPB
RING = 6
PW = PAIR * IB
FE = F + 1
XW = 2 * F + 2
XU = 2 * F + 1
BIG = float(2 ** 50)
SLOPE = 0.2
REST = 1.0 - SLOPE
CODES = 32480.0
CODE0 = 130.0
LO = 2048.0
EPS = 1e-5
FREE = 2
HALF = 512
HT = HALF // P
GROUP = 32


def gnn_program(nc, x_t, adj_t, ent_t, w_t, a_col, wt1, bias1, out):
    s_row = nc.dram_tensor("s_row", (TILES, P), F32, kind="Internal").ap()
    edges = nc.dram_tensor("edges", (OCTS * PAIRS, P, PW // 2), I16, kind="Internal").ap()
    x16_d = nc.dram_tensor("x16_d", (BLOCKS, P, IT * XW), F16, kind="Internal").ap()
    x1_d = nc.dram_tensor("x1_d", (BLOCKS, P, IT * F), F32, kind="Internal").ap()

    ctx = ExitStack()
    with ctx:
        def sb(name, shape, dt):
            return ctx.enter_context(nc.sbuf_tensor(name, shape, dt))

        def sem(name):
            return ctx.enter_context(nc.semaphore(name))

        off = sb("off", [P, RING * OCT * IB], BF16)
        adjb = sb("adjb", [P, PAIRS, PW], I32)
        edge = sb("edge", [P, PAIRS, PW], FP8)
        cand = sb("cand", [P, PW], I16)
        best = sb("best", [P, PW], I16)
        prob = sb("prob", [P, 2, IB], F32)
        ent = sb("ent", [P, TILES, FE], F32)
        s_bc = sb("s_bc", [P, 2 * IB], F32)
        rows = sb("rows", [GROUP + 3, 2, HALF], BF16)
        s_col = sb("s_col", [P, TILES], F32)
        code = sb("code", [P, TILES], F32)
        t_lo = sb("t_lo", [P, TILES], F32)
        t_hi = sb("t_hi", [P, TILES], F32)
        ident = sb("ident", [P, P], F32)
        ident16 = sb("ident16", [P, P], BF16)
        negbig = sb("negbig", [P, P], BF16)
        onesr = sb("onesr", [GROUP + 3, P], BF16)
        mean_e = sb("mean_e", [P, F], F32)
        wa = sb("wa", [P, 2, F], F32)
        small = sb("small", [P, 16], F32)
        stat = sb("stat", [P, 5, IT], F32)
        top = sb("top", [P, IT], BF16)
        shift = sb("shift", [P, IT], F32)
        mom = sb("mom", [P, 8, IT], F32)
        half = sb("half", [P, IT], F32)
        s_rows = sb("s_rows", [TILES, P], F32)
        ones = sb("ones", [P, P], F32)
        parts = sb("parts", [P, 2, 3, HT], BF16)
        partT = sb("partT", [3 * IT, P], BF16)
        maxes = sb("maxes", [P, 2, IT], F32)
        decay = sb("decay", [P, IT], F32)
        acc0 = sb("acc0", [P, IT, FE], F32)
        accT = sb("accT", [FE, IB], F32)
        xblk = sb("xblk", [P, IT, F], F32)
        ya = sb("ya", [P, IT, F], F32)
        yb = sb("yb", [P, IT, F], F32)
        x16 = sb("x16", [P, IT, XW], F16)
        wt_s = sb("wt_s", [P, F], F32)
        bias_s = sb("bias_s", [P, F], F32)
        w_s = sb("w_s", [F, F], F32)
        a_s = sb("a_s", [F, 2], F32)
        a_bc = sb("a_bc", [F, 2, P], F32)
        EW = OCT * IB
        e_all, tmp, x_all = [off[:, n * EW:n * EW + 2 * TILES * F].bitcast(F32)
                             .rearrange("p (t f) -> p t f", f=F) for n in range(RING - 3, RING)]
        slot2 = [(OCTS - RING + v // 2) % RING for v in range(OPB)]
        edge2 = [off[:, slot2[v] * EW + v % 2 * (EW // 2):slot2[v] * EW + (v % 2 + 1) * (EW // 2)].bitcast(FP8)
                 for v in range(OPB)]
        x16_all = adjb[:, 0:3, :].rearrange("p a b -> p (a b)")[:, 0:TILES * XW // 2].bitcast(F16)\
            .rearrange("p (b t w) -> p b t w", b=BLOCKS, t=IT)
        best16 = cand[:, 0:IB]
        agg = ent[:, 0:18, :].rearrange("p a b -> p (a b)")[:, 0:9 * XU].rearrange("p (t w) -> p t w", t=9)
        nx = prob[:, 0, :].rearrange("p (t w) -> p t w", t=IT)
        nxT = prob[:, 1, :]

        ps = ctx.enter_context(nc.psum_tensor("ps", [P, 8, HALF], F32))
        score = [ps[:, 2 * n:2 * n + 2, :].rearrange("p a b -> p (a b)") for n in range(2)]
        sums = ps[0:FE, 4:6, :].rearrange("p a b -> p (a b)")
        turn = ps[:, 6:8, :].rearrange("p a (t w) -> p (a t) w", w=P)
        turn_b = ps[:, 6, :].bitcast(BF16).rearrange("p (t w) -> p t w", w=P)
        turn16 = ps[0:3 * IT, 6, 0:HALF].bitcast(BF16)[:, 0:P]
        agg_ps = [ps[:, 3 * n:3 * n + 3, 0:3 * XU] for n in range(2)]

        ld_in = sem("ld_in")
        ld_x = sem("ld_x")
        ld_w = sem("ld_w")
        ld_1 = sem("ld_1")
        prep = sem("prep")
        pe_prep = sem("pe_prep")
        wa_in = sem("wa_in")
        s_step = sem("s_step")
        s_in = sem("s_in")
        ent_in = sem("ent_in")
        t_in = sem("t_in")
        srow_out = sem("srow_out")
        srow_tile = sem("srow_tile")
        pool_c = sem("pool_c")
        range_in = sem("range_in")
        range_out = sem("range_out")
        sbc_ld = sem("sbc_ld")
        adj_ld = [sem(f"adj_ld{k}") for k in range(PAIRS)]
        edge_st = [sem(f"edge_st{k}") for k in range(PAIRS)]
        off_in = sem("off_in")
        edge_due = sem("edge_due")
        cand_in = sem("cand_in")
        best_up = sem("best_up")
        best_clear = sem("best_clear")
        pair_done = sem("pair_done")
        oct_done = sem("oct_done")
        stat_step = sem("stat_step")
        epi_step = sem("epi_step")
        fin_step = sem("fin_step")
        epi_a = sem("epi_a")
        epi_b = sem("epi_b")
        best_in = sem("best_in")
        best_T = sem("best_T")
        parts_in = sem("parts_in")
        parts_T = sem("parts_T")
        partT_in = sem("partT_in")
        rows_ld = sem("rows_ld")
        shift_in = sem("shift_in")
        decay_in = sem("decay_in")
        relu_in = sem("relu_in")
        relu_due = sem("relu_due")
        score_in = sem("score_in")
        prob_in = sem("prob_in")
        acc_in = sem("acc_in")
        acc_T = sem("acc_T")
        xblk_ld = sem("xblk_ld")
        elu_in = sem("elu_in")
        elu_out = sem("elu_out")
        var_in = sem("var_in")
        var_out = sem("var_out")
        x16_in = sem("x16_in")
        x16_st = sem("x16_st")
        x1_st = sem("x1_st")
        x1_free = sem("x1_free")
        e2_ld = [sem(f"e2_ld{v}") for v in range(OPB)]
        x2_ld = [sem(f"x2_ld{b}") for b in range(BLOCKS)]
        e2_used = sem("e2_used")
        e2_seen = sem("e2_seen")
        agg_free = sem("agg_free")
        nx_ld = sem("nx_ld")
        nx_in = sem("nx_in")
        nx_x_in = sem("nx_x_in")
        nx_T = sem("nx_T")
        nxT_in = sem("nxT_in")
        y_ps = sem("y_ps")
        out_in = sem("out_in")
        out_st = sem("out_st")

        block = ctx.enter_context(nc.Block())

        def whole(ap):
            return ap.rearrange("a p n -> (a p) n")

        def over_f(ap):
            return ap.unsqueeze(2).to_broadcast([P, IT, F])

        def over_t(ap):
            return ap.unsqueeze(1).to_broadcast([P, IT, F])

        def pair_of(o, k):
            return off[:, bass.ds((o % RING) * (OCT * IB) + k * PW, PW)]

        def edge_load(sp, b, v):
            sp.dma_start(edge2[v].bitcast(I16).rearrange("p (k n) -> p k n", k=PAIRS),
                         edges[bass.ds(b * (OPB * PAIRS) + v * PAIRS, PAIRS)]
                         .rearrange("k p n -> p k n")).then_inc(e2_ld[v], 16)

        @block.sync
        def _(sp):
            sp.dma_start(w_s[:], w_t).then_inc(ld_w, 16)
            sp.dma_start(a_s[:], a_col).then_inc(ld_w, 16)
            sp.dma_start(e_all, ent_t.rearrange("p (t f) -> p t f", f=F)).then_inc(ld_in, 16)
            for k in range(PAIRS):
                sp.dma_start(adjb[:, k, :], adj_t[k]).then_inc(adj_ld[k], 16)
            sp.dma_start(x_all, x_t.rearrange("p (t f) -> p t f", f=F)).then_inc(ld_x, 16)
            sp.dma_start(wt_s[:], wt1).then_inc(ld_1, 16)
            sp.dma_start(bias_s[:], bias1.to_broadcast([P, F])).then_inc(ld_1, 16)

            def stream(o, first):
                for k in range(PAIRS):
                    sp.wait_ge(pair_done, o * PAIRS + (k + 1))
                    sp.dma_start(whole(edges[bass.ds(o * PAIRS + k, 1)]), edge[:, k, :].bitcast(I16))\
                      .then_inc(edge_st[k], 16)
                    if first:
                        sp.wait_ge(off_in, o * PAIRS + (k + 1))
                    sp.dma_start(adjb[:, k, :], whole(adj_t[bass.ds(o * PAIRS + (k + PAIRS), 1)]))\
                      .then_inc(adj_ld[k], 16)

            with sp.Fori(0, OPU) as o:
                stream(o, True)
            with sp.Fori(OPU, OCTS - 1) as o:
                stream(o, False)
            for k in range(PAIRS):
                sp.wait_ge(pair_done, (OCTS - 1) * PAIRS + k + 1)
                sp.dma_start(edges[(OCTS - 1) * PAIRS + k], edge[:, k, :].bitcast(I16)).then_inc(edge_st[k], 16)
            for b in range(BLOCKS):
                if b == BLOCKS - 1:
                    for k in range(PAIRS):
                        sp.wait_ge(edge_st[k], 16 * OCTS)
                    for v in range(OPB):
                        sp.wait_ge(oct_done, OCTS - RING + v // 2 + 1)
                        edge_load(sp, 0, v)
                sp.wait_ge(x16_st, 16 * (b + 1))
                sp.dma_start(x16_all[:, b], x16_d[b].rearrange("p (t w) -> p t w", t=IT)).then_inc(x2_ld[b], 16)
            with sp.Fori(1, BLOCKS) as b:
                for v in range(OPB):
                    sp.wait_ge(e2_used, (b - 1) * OPB + (v + 1))
                    edge_load(sp, b, v)

        @block.gpsimd
        def _(pool):
            pool.memset(ident[:], 0.0).then_inc(pool_c, 1)
            pool.memset(half[:], -0.5).then_inc(pool_c, 1)
            pool.wait_ge(pool_c, 2)
            pool.affine_select(out=ident[:], in_=ident[:], compare_op=ALU.not_equal, fill=1.0, base=0,
                               pattern=[[-1, P]], channel_multiplier=1).then_inc(pool_c, 1)
            pool.wait_ge(range_in, 2)
            pool.partition_all_reduce(small[:, 2:4], small[:, 0:2], P, RMAX).then_inc(range_out, 1)

            def load_s(b):
                pool.dma_start(s_bc[:, bass.ds((b % 2) * IB, IB)],
                               s_row.rearrange("(b t) p -> b (t p)", b=BLOCKS)[bass.ds(b, 1), :]
                               .to_broadcast([P, IB])).then_inc(sbc_ld, 16)

            def load_x(b):
                pool.dma_start(xblk[:].rearrange("p t f -> p (t f)"),
                               x_t.rearrange("p (b n) -> b p n", b=BLOCKS)[bass.ds(b, 1)]
                               .rearrange("a p n -> (a p) n")).then_inc(xblk_ld, 16)

            def power(b):
                pool.wait_ge(var_in, b + 1)
                pool.tensor_tensor(mom[:, 7, :], mom[:, 6, :], half[:, :], ALU.pow).then_inc(var_out, 1)

            def store_x1(b):
                pool.wait_ge(x16_in, b + 1)
                pool.dma_start(whole(x16_d[bass.ds(b, 1)]),
                               x16[:, :, :].rearrange("p t w -> p (t w)")).then_inc(x16_st, 16)
                pool.dma_start(whole(x1_d[bass.ds(b, 1)]),
                               ya[:, :, :].rearrange("p t f -> p (t f)")).then_inc(x1_st, 16)
                pool.wait_ge(x16_st, b * 16 + 16)
                pool.wait_ge(x1_st, b * 16 + 16)
                pool.sem_inc(x1_free, 1)

            pool.sem_inc(x1_free, 1)
            pool.wait_ge(ld_x, 16)
            pool.wait_ge(wa_in, 1)
            pool.tensor_tensor(x_all, x_all, wa[:, 0, :].unsqueeze(1).to_broadcast([P, TILES, F]), ALU.mult)\
                .then_inc(s_step, 1)
            width, steps = F // 2, 1
            while width > 1:
                pool.wait_ge(s_step, steps)
                pool.tensor_tensor(x_all[:, :, 0:width], x_all[:, :, 0:width], x_all[:, :, width:2 * width],
                                   ALU.add).then_inc(s_step, 1)
                width, steps = width // 2, steps + 1
            pool.wait_ge(s_step, steps)
            pool.tensor_tensor(s_col[:, :], x_all[:, :, 0:1].rearrange("p t o -> p (t o)"),
                               x_all[:, :, 1:2].rearrange("p t o -> p (t o)"), ALU.add).then_inc(s_in, 1)
            pool.wait_ge(srow_tile, 1)
            pool.dma_start(s_row, s_rows[:, :]).then_inc(srow_out, 16)
            pool.wait_ge(srow_out, 16)
            load_s(0)
            pool.wait_ge(rows_ld, 2 * 16)
            pool.wait_ge(sbc_ld, 16)
            load_s(1)
            load_x(0)

            def block_of(b, first, more):
                if not first:
                    store_x1(b - 2)
                    load_x(b - 1)
                if more:
                    pool.wait_ge(sbc_ld, b * 16 + 16)
                    pool.wait_ge(oct_done, b * OPB)
                    load_s(b + 1)
                power(b - 1)

            block_of(1, True, True)
            with pool.Fori(2, BLOCKS - 1) as b:
                block_of(b, False, True)
            block_of(BLOCKS - 1, False, False)
            store_x1(BLOCKS - 2)
            load_x(BLOCKS - 1)
            power(BLOCKS - 1)
            store_x1(BLOCKS - 1)
            pool.wait_ge(x1_st, 16 * BLOCKS)
            with pool.Fori(0, BLOCKS) as b:
                power(b + BLOCKS)

        @block.vector
        def _(dve):
            V = nc.vector
            at = [0]

            def link(ins, sem_, base=0):
                at[0] += 1
                ins.then_inc(sem_, 1)
                dve.wait_ge(sem_, base + at[0])

            def clear_best(b):
                V.memset(best[:].bitcast(I32), 0).then_inc(best_clear, 1)
                dve.wait_ge(best_clear, b + 1)

            V.memset(a_bc[:].rearrange("p a b -> p (a b)"), 1.0).then_inc(prep, 1)
            V.memset(onesr[:], 1.0).then_inc(prep, 1)
            V.memset(ones[:], 1.0).then_inc(prep, 1)
            V.memset(ent[:, :, F:FE], 1.0).then_inc(prep, 1)
            V.memset(x16[:, :, 2 * F:2 * F + 1], 1.0).then_inc(prep, 1)
            V.memset(x16[:, :, 2 * F + 1:XW], 0.0).then_inc(prep, 1)
            clear_best(0)
            at[0] = 6
            dve.wait_ge(pool_c, 3)
            V.tensor_scalar(negbig[:], ident[:], -BIG, None, ALU.mult).then_inc(prep, 1)
            V.tensor_copy(ident16[:], ident[:]).then_inc(prep, 1)
            at[0] = 8
            dve.wait_ge(prep, 8)
            dve.wait_ge(ld_w, 32)
            for k in range(2):
                link(V.tensor_scalar(a_bc[:, k, :], a_bc[:, k, :], a_s[:, k:k + 1], None, ALU.mult), prep)
            dve.wait_ge(pe_prep, 1)
            V.tensor_copy(wa[:], ps[:, 6, 0:2 * F].rearrange("p (k f) -> p k f", k=2)).then_inc(wa_in, 1)
            dve.wait_ge(wa_in, 1)
            dve.wait_ge(ld_in, 16)
            link(V.tensor_tensor(tmp, e_all, wa[:, 1, :].unsqueeze(1).to_broadcast([P, TILES, F]), ALU.mult), prep)
            link(V.tensor_reduce(t_lo[:], tmp, AX.X, ALU.add), prep)
            V.tensor_reduce(small[:, 0:1], t_lo[:], AX.X, ALU.max).then_inc(range_in, 1)
            link(V.tensor_reduce(small[:, 8:9], t_lo[:], AX.X, ALU.min), prep)
            V.tensor_scalar(small[:, 1:2], small[:, 8:9], -1.0, None, ALU.mult).then_inc(range_in, 1)
            dve.wait_ge(range_out, 1)
            link(V.tensor_tensor(small[:, 4:5], small[:, 2:3], small[:, 3:4], ALU.add), prep)
            link(V.tensor_scalar(small[:, 5:6], small[:, 4:5], 1.0 / CODES, 1e-30, ALU.mult, ALU.max), prep)
            link(V.reciprocal(small[:, 6:7], small[:, 5:6]), prep)
            link(V.scalar_tensor_tensor(small[:, 9:10], small[:, 5:6], CODE0 - 1.0, small[:, 3:4],
                                        ALU.mult, ALU.add), prep)
            link(V.tensor_scalar(small[:, 7:8], small[:, 9:10], -1.0, None, ALU.mult), prep)
            link(V.tensor_scalar(code[:], t_lo[:], small[:, 3:4], small[:, 6:7], ALU.add, ALU.mult), prep)
            link(V.tensor_scalar(code[:], code[:], CODE0, None, ALU.add), prep)
            link(V.tensor_scalar(t_hi[:], t_lo[:], REST, None, ALU.mult), prep)
            V.tensor_scalar(t_lo[:], t_lo[:], SLOPE, None, ALU.mult).then_inc(t_in, 1)

            def sweep_a(o, c, oo, ring_free, first=False, own=True):
                for k in range(PAIRS):
                    if ring_free:
                        dve.wait_ge(score_in, (o - RING) * OCT + (k + 1) * PAIR)
                    if not first:
                        dve.wait_ge(edge_st[k], o * 16)
                    dve.wait_ge(adj_ld[k], o * 16 + 16)
                    pair = pair_of(o, k)
                    if own:
                        V.tensor_scalar(pair, adjb[:, k, :], 0.0, None, ALU.is_le).then_inc(off_in, 1)
                    elif not first:
                        dve.sem_inc(edge_due, 1)
                    V.tensor_scalar(edge[:, k, :], adjb[:, k, :], 1.0, None, ALU.is_equal,
                                    saturate=False).then_inc(pair_done, 1)
                    dve.wait_ge(off_in, o * PAIRS + (k + 1))
                    if not first or k:
                        dve.wait_ge(best_up, o * PAIRS + k)
                    for n in range(PAIR):
                        tile_off = off[:, bass.ds((o % RING) * (OCT * IB) + (k * PAIR + n) * IB, IB)]
                        jt = (c * OPU + oo) * OCT + (k * PAIR + n)
                        V.tensor_scalar(cand[:, n * IB:(n + 1) * IB], tile_off, 0.0,
                                        code[:, bass.ds(jt, 1)], ALU.is_equal, ALU.mult).then_inc(cand_in, 1)
                    dve.wait_ge(cand_in, o * OCT + (k + 1) * PAIR)
                    V.tensor_tensor(best[:], best[:], cand[:], ALU.max).then_inc(best_up, 1)

            STATS = 8

            def stats(b, c, meanwhile=None):
                u = 2 * b + c
                at[0] = 0

                def step(ins):
                    link(ins, stat_step, u * STATS)

                dve.wait_ge(best_up, (u + 1) * (OPU * PAIRS))
                V.tensor_tensor(best16, best[:, 0:IB], best[:, IB:PW], ALU.max).then_inc(best_in, 1)
                if meanwhile:
                    meanwhile()
                at[0] = 0
                dve.wait_ge(best_T, u + 1)
                step(V.tensor_reduce(top[:, :], turn_b, AX.X, ALU.max))
                step(V.tensor_scalar(stat[:, 1, :], top[:, :].bitcast(I16), small[:, 5:6], small[:, 7:8],
                                     ALU.mult, ALU.add))
                s_b = s_col[:, bass.ds(b * IT, IT)]
                step(V.tensor_tensor(stat[:, 2, :], stat[:, 1, :], s_b, ALU.add))
                step(V.scalar_tensor_tensor(maxes[:, c, :], stat[:, 2, :], SLOPE, stat[:, 2, :],
                                            ALU.mult, ALU.max))
                step(V.scalar_tensor_tensor(stat[:, 3, :], s_b, SLOPE, maxes[:, c, :],
                                            ALU.mult, ALU.subtract))
                val, rest = [stat[:, n, :].rearrange("p (h t) -> p h t", h=2) for n in (3, 4)]
                step(V.tensor_copy(parts[:, :, 0, :], val))
                step(V.tensor_tensor(rest, val, parts[:, :, 0, :], ALU.subtract))
                step(V.tensor_copy(parts[:, :, 1, :], rest))
                V.tensor_tensor(parts[:, :, 2, :], rest, parts[:, :, 1, :], ALU.subtract).then_inc(parts_in, 1)
                if c == 1:
                    V.tensor_tensor(shift[:], maxes[:, 0, :], maxes[:, 1, :], ALU.subtract).then_inc(shift_in, 1)
                assert at[0] == STATS

            def evac0(b):
                dve.wait_ge(acc_T, 2 * b + 2)
                V.tensor_copy(acc0[:, :, :], turn[:, :, 0:FE]).then_inc(epi_a, 1)

            EPI = 16

            def evac1(b):
                at[0] = 0

                def step(ins):
                    link(ins, epi_step, b * EPI)

                dve.wait_ge(epi_a, b + 1)
                dve.wait_ge(decay_in, b + 1)
                step(V.tensor_tensor(acc0[:, :, :], acc0[:, :, :],
                                     decay[:, :].unsqueeze(2).to_broadcast([P, IT, FE]), ALU.mult))
                dve.wait_ge(acc_T, 2 * b + 3)
                step(V.tensor_tensor(acc0[:, :, :], turn[:, :, 0:FE], acc0[:, :, :], ALU.add))
                den = acc0[:, :, F:FE].rearrange("p t o -> p (t o)")
                step(V.tensor_scalar(mom[:, 0, :], den, 0.0, None, ALU.is_equal))
                step(V.tensor_tensor(mom[:, 1, :], den, mom[:, 0, :], ALU.add))
                step(V.reciprocal(mom[:, 2, :], mom[:, 1, :]))
                dve.wait_ge(x1_free, b + 1)
                step(V.tensor_tensor(ya[:], acc0[:, :, 0:F], over_f(mom[:, 2, :]), ALU.mult))
                step(V.tensor_tensor(yb[:], over_t(mean_e[:]), over_f(mom[:, 0, :]), ALU.mult))
                step(V.tensor_tensor(ya[:], ya[:], yb[:], ALU.add))
                dve.wait_ge(xblk_ld, b * 16 + 16)
                step(V.tensor_tensor(ya[:], ya[:], xblk[:], ALU.add))
                V.tensor_scalar(yb[:], ya[:], 0.0, None, ALU.min).then_inc(elu_in, 1)

            def norm(step, b):
                step(V.tensor_reduce(mom[:, 3, :], ya[:], AX.X, ALU.add))
                step(V.tensor_scalar(mom[:, 4, :], mom[:, 3, :], 1.0 / F, None, ALU.mult))
                step(V.tensor_tensor(ya[:], ya[:], over_f(mom[:, 4, :]), ALU.subtract))
                step(V.tensor_tensor(yb[:], ya[:], ya[:], ALU.mult))
                step(V.tensor_reduce(mom[:, 5, :], yb[:], AX.X, ALU.add))
                V.tensor_scalar(mom[:, 6, :], mom[:, 5, :], 1.0 / F, EPS, ALU.mult, ALU.add).then_inc(var_in, 1)

            def add_elu(b):
                at[0] = 9

                def step(ins):
                    link(ins, epi_step, b * EPI)

                dve.wait_ge(elu_out, b + 1)
                step(V.scalar_tensor_tensor(ya[:], ya[:], 0.0, yb[:], ALU.max, ALU.add))
                step(V.scalar_tensor_tensor(ya[:], ya[:], -1.0, xblk[:], ALU.add, ALU.add))
                norm(step, b)
                assert at[0] == EPI

            def split_x1(b):
                dve.wait_ge(var_out, b + 1)
                V.tensor_tensor(ya[:], ya[:], over_f(mom[:, 7, :]), ALU.mult).then_inc(epi_b, 1)
                dve.wait_ge(epi_b, b * 3 + 1)
                V.tensor_copy(x16[:, :, 0:F], ya[:]).then_inc(epi_b, 1)
                dve.wait_ge(epi_b, b * 3 + 2)
                V.tensor_tensor(yb[:], ya[:], x16[:, :, 0:F], ALU.subtract).then_inc(epi_b, 1)
                dve.wait_ge(epi_b, b * 3 + 3)
                V.tensor_scalar(x16[:, :, F:2 * F], yb[:], LO, None, ALU.mult).then_inc(x16_in, 1)

            sweep_a(0, 0, 0, False, True, False)
            with dve.Fori(1, OPU - 1) as oo:
                sweep_a(oo, 0, oo, False, False, False)
            dve.wait_ge(pe_prep, 2)
            link(V.tensor_reduce(mean_e[:], ps[:, 7, :].rearrange("p (t f) -> p f t", f=F), AX.X, ALU.add), prep)
            link(V.tensor_scalar(mean_e[:], mean_e[:], 1.0 / N, None, ALU.mult), prep)
            sweep_a(OPU - 1, 0, OPU - 1, False, False, False)
            dve.wait_ge(s_in, 1)
            stats(0, 0)
            for oo in range(OPU):
                sweep_a(OPU + oo, 1, oo, OPU + oo >= RING)
            stats(0, 1)
            clear_best(1)

            def block_of(b, first):
                with dve.Fori(0, 2) as oo:
                    sweep_a(b * OPB + oo, 0, oo, True)
                evac0(b - 1)
                with dve.Fori(2, OPU) as oo:
                    sweep_a(b * OPB + oo, 0, oo, True)
                dve.wait_ge(epi_a, b)
                stats(b, 0, None if first else lambda: split_x1(b - 2))
                with dve.Fori(0, 2) as oo:
                    sweep_a(b * OPB + OPU + oo, 1, oo, True)
                evac1(b - 1)
                with dve.Fori(2, OPU) as oo:
                    sweep_a(b * OPB + OPU + oo, 1, oo, True)

                def meanwhile():
                    dve.wait_ge(best_in, 2 * b + 2)
                    clear_best(b + 1)
                    add_elu(b - 1)

                stats(b, 1, meanwhile)

            block_of(1, True)
            with dve.Fori(2, BLOCKS) as b:
                block_of(b, False)
            last = BLOCKS - 1
            split_x1(last - 1)
            evac0(last)
            dve.wait_ge(prob_in, BLOCKS * TILES + FREE)
            V.memset(agg_ps[0], 0.0).then_inc(agg_free, 1)
            dve.wait_ge(acc_in, 2 * BLOCKS)
            V.memset(agg_ps[1], 0.0).then_inc(agg_free, 1)
            evac1(last)
            add_elu(last)
            split_x1(last)

            FIN = 10

            def layer1_end(b, n, first=False):
                at[0] = 0

                def step(ins):
                    link(ins, fin_step, b * FIN)

                dve.wait_ge(e2_used, (b + 1) * OPB)
                step(V.tensor_copy(agg.rearrange("p (a t) w -> p a (t w)", a=3), agg_ps[n]))
                step(V.reciprocal(mom[:, 0, :], agg[:, 0:IT, 2 * F:XU].rearrange("p t o -> p (t o)")))
                if first:
                    dve.wait_ge(x1_st, 16 * BLOCKS)
                else:
                    dve.wait_ge(out_st, b * 16)
                step(V.scalar_tensor_tensor(ya[:], agg[:, 0:IT, F:2 * F], 1.0 / LO, agg[:, 0:IT, 0:F],
                                            ALU.mult, ALU.add))
                V.tensor_tensor(nx[:, :, 0:F], ya[:], over_f(mom[:, 0, :]), ALU.mult).then_inc(nx_in, 1)
                V.memset(agg_ps[n], 0.0).then_inc(agg_free, 1)
                dve.wait_ge(nx_ld, b * 16 + 16)
                step(V.tensor_tensor(yb[:], xblk[:], over_t(bias_s[:]), ALU.add))
                dve.wait_ge(y_ps, b + 1)
                step(V.tensor_tensor(ya[:], ps[:, 6, :].rearrange("p (t f) -> p t f", f=F), yb[:], ALU.add))
                norm(step, b + BLOCKS)
                dve.wait_ge(var_out, b + (BLOCKS + 1))
                V.tensor_tensor(ya[:], ya[:], over_f(mom[:, 7, :]), ALU.mult).then_inc(out_in, 1)
                assert at[0] == FIN

            dve.wait_ge(ld_1, 32)
            layer1_end(0, 0, True)
            layer1_end(1, 1)
            with dve.Fori(1, BLOCKS // 2) as two:
                for n in range(2):
                    layer1_end(two * 2 + n, n)

        @block.scalar
        def _(act):
            A = nc.scalar

            def relu(b, c, oo, t):
                act.wait_ge(prob_in, (b * OPB + (c * OPU + oo)) * OCT + (t + 1))
                if isinstance(oo, int):
                    act.sem_inc(relu_due, 1)
                jt = (c * OPU + oo) * OCT + t
                A.activation(score[t % 2], s_bc[:, bass.ds((b % 2) * IB, IB)], ACT.Relu, scale=REST,
                             bias=t_hi[:, bass.ds(jt, 1)]).then_inc(relu_in, 1)

            def octet(b, c, oo, after, then):
                for t in range(OCT):
                    act.wait_ge(score_in, (b * OPB + (c * OPU + oo)) * OCT + (t + 1))
                    jt = (c * OPU + oo) * OCT + t
                    A.activation(prob[:, t % 2, :], score[t % 2], ACT.Exp,
                                 bias=t_lo[:, bass.ds(jt, 1)]).then_inc(prob_in, 1)
                    if t in then:
                        then[t]()
                    if t + 2 < OCT:
                        relu(b, c, oo, t + 2)
                    elif after:
                        if t + 2 == OCT and after[1] == 0 and c == 1:
                            act.wait_ge(sbc_ld, after[0] * 16 + 16)
                        relu(*after, t + 2 - OCT)

            def evac(u):
                act.wait_ge(oct_done, u * OPU + OPU)
                act.wait_ge(acc_T, u + 1)
                A.copy(accT[:, :], sums).then_inc(acc_in, 1)

            def take_parts(u, c):
                act.wait_ge(parts_T, u + 1)
                if not (isinstance(u, int) and u == 0):
                    act.wait_ge(rows_ld, u * 32)
                A.copy(partT[:, :], turn16).then_inc(partT_in, 1)
                act.wait_ge(partT_in, u + 1)
                for h in range(2):
                    act.dma_start(rows[h * GROUP:h * GROUP + 3, c, :].rearrange("k (t p) -> k t p", p=P),
                                  partT[h * 3 * HT:(h + 1) * 3 * HT, :]).then_inc(rows_ld, 16)

            def exp_decay(b):
                act.wait_ge(shift_in, b + 1)
                A.activation(decay[:], shift[:], ACT.Exp).then_inc(decay_in, 1)

            def exp_elu(b):
                act.wait_ge(elu_in, b + 1)
                A.activation(yb[:], yb[:], ACT.Exp).then_inc(elu_out, 1)

            def unit(b, c, after):
                u = 2 * b + c
                if isinstance(u, int) and u == 0:
                    octet(b, c, 0, (b, c, 1), {})
                else:
                    octet(b, c, 0, (b, c, 1), {0: lambda: evac(u - 1)})
                if c == 0 and not (isinstance(b, int) and b == 0):
                    octet(b, c, 1, (b, c, 2), {})
                    octet(b, c, 2, (b, c, 3), {0: lambda: exp_elu(b - 1)})
                else:
                    with act.Fori(1, OPU - 1) as oo:
                        octet(b, c, oo, (b, c, oo + 1), {})
                then = {4 if isinstance(u, int) and u == 0 else 2: lambda: take_parts(u + 1, 1 - c)} if after else {}
                if c == 1:
                    then[0] = lambda: exp_decay(b)
                octet(b, c, 3, after, then)

            act.sem_inc(prob_in, FREE)
            act.wait_ge(ld_in, 16)
            A.copy(ent[:, :, 0:F], e_all).then_inc(ent_in, 1)

            def make_off(o):
                for k in range(PAIRS):
                    act.wait_ge(adj_ld[k], o * 16 + 16)
                    A.activation(pair_of(o, k), adjb[:, k, :], ACT.Relu, scale=-1.0, bias=1.0).then_inc(off_in, 1)

            make_off(0)
            make_off(1)
            act.wait_ge(pe_prep, 3)
            A.copy(s_rows[:, :], ps[0:TILES, 6, 0:P]).then_inc(srow_tile, 1)
            make_off(2)
            act.wait_ge(t_in, 1)
            make_off(3)
            act.wait_ge(sbc_ld, 16)
            last = BLOCKS - 1
            relu(0, 0, 0, 0)
            relu(0, 0, 0, 1)
            take_parts(0, 0)
            unit(0, 0, (0, 1, 0))
            with act.Fori(0, last) as b:
                unit(b, 1, (b + 1, 0, 0))
                unit(b + 1, 0, (b + 1, 1, 0))
            unit(last, 1, None)
            evac(2 * last + 1)
            exp_elu(last)

            def layer1(b, first=False):
                if not first:
                    act.wait_ge(out_in, b)
                    act.dma_start(whole(out[bass.ds(b - 1, 1)]), ya[:].rearrange("p t f -> p (t f)"))\
                        .then_inc(out_st, 16)
                act.dma_start(xblk[:].rearrange("p t f -> p (t f)"), whole(x1_d[bass.ds(b, 1)]))\
                    .then_inc(nx_ld, 16)
                act.wait_ge(nx_ld, b * 16 + 16)
                A.copy(nx[:, :, F:2 * F], xblk[:]).then_inc(nx_x_in, 1)
                act.wait_ge(nx_T, b + 1)
                A.copy(nxT, turn.rearrange("p t w -> p (t w)")).then_inc(nxT_in, 1)

            act.wait_ge(x1_st, 16 * BLOCKS)
            layer1(0, True)
            with act.Fori(1, BLOCKS) as b:
                layer1(b)
            act.wait_ge(out_in, BLOCKS)
            act.dma_start(out[BLOCKS - 1], ya[:].rearrange("p t f -> p (t f)")).then_inc(out_st, 16)
            act.wait_ge(out_st, 16 * BLOCKS)

        @block.tensor
        def _(pe):
            M = nc.tensor.matmul
            pe.wait_ge(prep, 10)
            for k in range(2):
                ins = M(ps[:, 6, k * F:(k + 1) * F], a_bc[:, k, :], w_s[:, :], start=True, stop=True)
            ins.then_inc(pe_prep, 1)
            pe.wait_ge(ld_in, 16)
            for n in range(TILES * F // HALF):
                ins = M(ps[:, 7, :], ones[:, :], e_all[:, n * (HALF // F):(n + 1) * (HALF // F), :]
                        .rearrange("p t f -> p (t f)"), start=n == 0, stop=n == TILES * F // HALF - 1)
            ins.then_inc(pe_prep, 1)
            for n in range(2):
                for h in range(2):
                    for q in range(HALF // P):
                        at = h * HALF + q * P
                        ins = M(score[n][:, at:at + P], ident16[:, :], negbig[:, :], start=q == 0, stop=True,
                                skip_group_check=True)
            pe.wait_ge(wa_in, 1)
            pe.wait_ge(s_in, 1)
            nc.tensor.transpose(ps[0:TILES, 6, 0:P], s_col[:, :], ident[:, :]).then_inc(pe_prep, 1)

            def turn_best(u):
                pe.wait_ge(best_in, u + 1)
                for t in range(IT):
                    ins = nc.tensor.transpose(turn_b[:, t, :], best16[:, t * P:(t + 1) * P].bitcast(BF16), ident16[:, :])
                ins.then_inc(best_T, 1)

            def turn_parts(u):
                pe.wait_ge(parts_in, u + 1)
                nc.tensor.transpose(turn16, parts[:, :, :, :].rearrange("p h k t -> p (h k t)"),
                                    ident16[:, :]).then_inc(parts_T, 1)

            def turn_sums(u):
                pe.wait_ge(acc_in, u + 1)
                for t in range(IT):
                    ins = nc.tensor.transpose(turn[:, t, 0:FE], accT[:, t * P:(t + 1) * P], ident[0:FE, 0:FE])
                ins.then_inc(acc_T, 1)

            def add(b, c, oo, t):
                o = b * OPB + (c * OPU + oo)
                pe.wait_ge(relu_in, o * OCT + (t + 1))
                for h in range(2):
                    M(score[t % 2][:, h * HALF:(h + 1) * HALF], negbig[:, :],
                      off[:, bass.ds((o % RING) * (OCT * IB) + t * IB + h * HALF, HALF)],
                      start=False, stop=True, skip_group_check=True)
                for h in range(2):
                    g = h * GROUP
                    ins = M(score[t % 2][:, h * HALF:(h + 1) * HALF], onesr[g:g + 3, :],
                            rows[g:g + 3, c, :], start=False, stop=True,
                            skip_group_check=True)
                ins.then_inc(score_in, 1)

            def octet(b, c, oo, after, then, fresh=False):
                o = b * OPB + (c * OPU + oo)
                for t in range(OCT):
                    if t + 1 < OCT:
                        add(b, c, oo, t + 1)
                    elif after:
                        if oo == last_oo:
                            pe.wait_ge(rows_ld, (2 * b + c) * 32 + 64)
                        add(*after, 0)
                    if fresh and t == 0 and not (isinstance(b, int) and 2 * b + c == 0):
                        pe.wait_ge(acc_in, 2 * b + c)
                    pe.wait_ge(prob_in, o * OCT + (t + 1 + FREE))
                    jt = (c * OPU + oo) * OCT + t
                    for h in range(2):
                        ins = M(sums[:, h * HALF:(h + 1) * HALF],
                                ent[:, jt, :], prob[:, t % 2, h * HALF:(h + 1) * HALF],
                                start=fresh and t == 0, stop=True, skip_group_check=True)
                    if t == OCT - 1:
                        ins.then_inc(oct_done, 1)
                    if t in then:
                        then[t]()

            last_oo = OPU - 1

            def unit(b, c, after):
                u = 2 * b + c
                first = isinstance(u, int) and u == 0
                late = 2 if first else 0
                octet(b, c, 0, (b, c, 1), {} if first else {3: lambda: turn_sums(u - 1)}, fresh=True)
                for oo in range(1, last_oo):
                    octet(b, c, oo, (b, c, oo + 1),
                          {5 + late: lambda: turn_best(u + 1)} if after and oo == last_oo - 1 else {})
                octet(b, c, last_oo, after, {late: lambda: turn_parts(u + 1)} if after else {})

            pe.sem_inc(acc_T, 1)
            pe.wait_ge(srow_tile, 1)

            def keep_busy(count):
                for n in range(count):
                    M(turn[:, 4:8, :].rearrange("p t w -> p (t w)"), negbig[:, :], off[:, 0:HALF],
                      start=True, stop=True, skip_group_check=True)

            turn_best(0)
            keep_busy(9)
            turn_parts(0)
            keep_busy(9)
            last = BLOCKS - 1
            pe.wait_ge(ent_in, 1)
            pe.wait_ge(rows_ld, 32)
            add(0, 0, 0, 0)
            unit(0, 0, (0, 1, 0))
            with pe.Fori(0, last) as b:
                unit(b, 1, (b + 1, 0, 0))
                unit(b + 1, 0, (b + 1, 1, 0))
            unit(last, 1, None)
            pe.wait_ge(epi_a, BLOCKS)
            turn_sums(2 * last + 1)

            def edges_of(b, n, then, first=False):
                pe.wait_ge(agg_free, b + 1)
                for v in range(OPB):
                    pe.wait_ge(e2_ld[v], b * 16 + 16)
                    pe.sem_inc(e2_seen, 1)
                    if first:
                        pe.wait_ge(x2_ld[v], 16)
                    for t in range(OCT):
                        for m in range(IT):
                            ins = M(agg_ps[n][:, m // 3, (m % 3) * XU:(m % 3 + 1) * XU],
                                    edge2[v][:, t * IB + m * P:t * IB + (m + 1) * P],
                                    x16_all[:, v, t, 0:XU], start=False, stop=True, skip_group_check=True)
                    ins.then_inc(e2_used, 1)
                    if v in then:
                        then[v]()

            def turn_nx(b):
                pe.wait_ge(nx_in, b + 1)
                pe.wait_ge(nx_x_in, b + 1)
                for m in range(IT):
                    ins = nc.tensor.transpose(turn[:, m, :], nx[:, m, :], ident[:, :])
                ins.then_inc(nx_T, 1)

            def apply_weight(b):
                pe.wait_ge(nxT_in, b + 1)
                for m in range(IT):
                    ins = M(ps[:, 6, m * F:(m + 1) * F], nxT[:, m * P:(m + 1) * P], wt_s[:, :],
                            start=True, stop=True)
                ins.then_inc(y_ps, 1)

            def behind(b):
                return {3: lambda: turn_nx(b), 5: lambda: apply_weight(b)}

            edges_of(0, 0, {}, True)
            with pe.Fori(0, BLOCKS // 2 - 1) as two:
                edges_of(two * 2 + 1, 1, behind(two * 2))
                edges_of(two * 2 + 2, 0, behind(two * 2 + 1))
            edges_of(BLOCKS - 1, 1, behind(BLOCKS - 2))
            turn_nx(BLOCKS - 1)
            apply_weight(BLOCKS - 1)


def kernel(x, adj, L0_gnn_entity_embs, L0_gnn_W, L0_gnn_a, L1_gnn_weight, L1_gnn_bias):
    import numpy as np
    import concourse.bacc as bacc
    from concourse.bass_utils import run_bass_kernel_spmd

    def tiled(a):
        return np.ascontiguousarray(np.asarray(a).reshape(TILES, P, F).transpose(1, 0, 2)).reshape(P, TILES * F)

    adj_t = np.asarray(adj).reshape(BLOCKS, IB, OPB, PAIRS, PAIR, P).transpose(0, 2, 3, 5, 4, 1)
    arrays = {
        "x_t": tiled(x),
        "adj_t": np.ascontiguousarray(adj_t).reshape(OCTS * PAIRS, P, PW),
        "ent_t": tiled(L0_gnn_entity_embs),
        "w_t": np.ascontiguousarray(np.asarray(L0_gnn_W).T),
        "a_col": np.ascontiguousarray(np.asarray(L0_gnn_a).reshape(2, F).T),
        "wt1": np.ascontiguousarray(np.asarray(L1_gnn_weight)),
        "bias1": np.ascontiguousarray(np.asarray(L1_gnn_bias).reshape(1, F)),
    }
    nc = bacc.Bacc("TRN2", target_bir_lowering=False, num_devices=1)
    args = [nc.dram_tensor(k, a.shape, mybir.dt.from_np(a.dtype), kind="ExternalInput").ap()
            for k, a in arrays.items()]
    out = nc.dram_tensor("out", (BLOCKS, P, IT * F), F32, kind="ExternalOutput").ap()
    gnn_program(nc, *args, out)
    got = run_bass_kernel_spmd(nc, [arrays], core_ids=[0]).results[0]["out"]
    return np.ascontiguousarray(np.asarray(got).reshape(BLOCKS, P, IT, F).transpose(0, 2, 1, 3)).reshape(N, F)
```
